# Optimizing a Trainium2 kernel written in Bass

```python
import numpy as np
import jax
import jax.numpy as jnp

def _softmax(x, axis=-1):
    return jax.nn.softmax(x, axis=axis)

def _gelu(x):
    return jax.nn.gelu(x, approximate=True)

def _silu(x):
    return jax.nn.silu(x)

def _sigmoid(x):
    return jax.nn.sigmoid(x)

def _layernorm(x, axis=-1, eps=1e-05):
    m = jnp.mean(x, axis=axis, keepdims=True)
    v = jnp.var(x, axis=axis, keepdims=True)
    return (x - m) / jnp.sqrt(v + eps)

def _scatter_add(tgt, idx, src, axis=0):
    return tgt.at[idx].add(src)

def _segment_sum(src, seg, n):
    return jax.ops.segment_sum(src, seg, n)
kernel_name = 'mk_hybrid_d2_jaxref_r8_a5ae06'

def setup_inputs(seed: int=0):
    np.random.seed(seed)
    _w = jnp.asarray

    def _L0_attn_a_setup():
        import jax, jax.numpy as jnp
        import numpy as np
        from math import sqrt
        D_MODEL = 128
        N_HEADS = 16
        key = jax.random.key(seed)
        k1, k2, k3 = jax.random.split(key, 3)
        B, T, C = (4, 256, D_MODEL)
        x = jax.random.normal(k1, (B, T, C), dtype=jnp.float32)
        w_qkv = jax.random.normal(k2, (C, 3 * C), dtype=jnp.float32) * (1.0 / sqrt(C))
        w_out = jax.random.normal(k3, (C, C), dtype=jnp.float32) * (1.0 / sqrt(C))
        b_out = jnp.zeros((C,), dtype=jnp.float32)
        return {'x': x, 'w_qkv': w_qkv, 'w_out': w_out, 'b_out': b_out}
    _L0_attn_a_in = _L0_attn_a_setup()

    def _L0_attn_b_setup():
        import jax, jax.numpy as jnp
        import numpy as np
        EMBED_DIM = 128
        NUM_HEADS = 16
        HEAD_DIM = EMBED_DIM // NUM_HEADS
        NUM_DECAYS = 2
        BATCH = 2
        SEQ = 256
        W_SCALE = 0.02
        key = jax.random.key(seed)
        ks = jax.random.split(key, 12)
        d = EMBED_DIM
        inp = {'x': jax.random.normal(ks[0], (BATCH, SEQ, d), dtype=jnp.float32), 'Wq': jax.random.normal(ks[1], (d, d), dtype=jnp.float32) * W_SCALE, 'bq': jnp.zeros((d,), dtype=jnp.float32), 'Wk': jax.random.normal(ks[2], (d, d), dtype=jnp.float32) * W_SCALE, 'bk': jnp.zeros((d,), dtype=jnp.float32), 'Wv': jax.random.normal(ks[3], (d, d), dtype=jnp.float32) * W_SCALE, 'bv': jnp.zeros((d,), dtype=jnp.float32), 'Wo': jax.random.normal(ks[4], (d, d), dtype=jnp.float32) * W_SCALE, 'bo': jnp.zeros((d,), dtype=jnp.float32), 'decay_params': jax.random.uniform(ks[5], (NUM_HEADS, NUM_DECAYS), dtype=jnp.float32), 'mix_weights': jax.random.normal(ks[6], (NUM_HEADS, NUM_DECAYS), dtype=jnp.float32)}
        return inp
    _L0_attn_b_in = _L0_attn_b_setup()

    def _L0_ffn_setup():
        import jax, jax.numpy as jnp
        import numpy as np
        D, H, E, K = (128, 128, 8, 2)

        def _moe(x, router_w, w_in, b_in, w_out, b_out):
            B, S, Dm = x.shape
            T = B * S
            x2 = x.reshape(T, Dm)
            logits = x2 @ router_w
            probs = jax.nn.softmax(logits, axis=-1)
            top_p, top_e = jax.lax.top_k(probs, K)
            flat_e = top_e.reshape(-1)
            flat_p = top_p.reshape(-1)
            tok = jnp.repeat(jnp.arange(T), K)
            order = jnp.argsort(flat_e)
            se, sp, st = (flat_e[order], flat_p[order], tok[order])
            xd = x2[st]
            N = xd.shape[0]
            h = jnp.zeros((N, H), x.dtype)
            for e in range(E):
                m = (se == e)[:, None]
                h = h + jnp.where(m, jax.nn.gelu(xd @ w_in[e] + b_in[e]), 0.0)
            y = jnp.zeros((N, Dm), x.dtype)
            for e in range(E):
                m = (se == e)[:, None]
                y = y + jnp.where(m, h @ w_out[e] + b_out[e], 0.0)
            y = y * sp[:, None]
            out = jnp.zeros((T, Dm), x.dtype).at[st].add(y)
            return out.reshape(B, S, Dm)
        key = jax.random.key(seed)
        ks = jax.random.split(key, 5)
        s = lambda k, shape, scale: jax.random.normal(k, shape, dtype=jnp.float32) * scale
        return {'input_batch': s(ks[0], (2, 64, D), 1.0), 'router_w': s(ks[1], (D, E), D ** (-0.5)), 'w_in': s(ks[2], (E, D, H), D ** (-0.5)), 'b_in': jnp.zeros((E, H), jnp.float32), 'w_out': s(ks[3], (E, H, D), H ** (-0.5)), 'b_out': jnp.zeros((E, D), jnp.float32)}
    _L0_ffn_in = _L0_ffn_setup()

    def _L1_attn_a_setup():
        import jax, jax.numpy as jnp
        import numpy as np
        import math
        _DENSE_LOCAL_W = 64
        _DYADIC = [96, 128, 192, 32, 48, 64, 96, 128, 192]
        OFFSETS = sorted(set(range(0, _DENSE_LOCAL_W + 1)) | set(_DYADIC))
        B, N, D, H = (1, 256, 128, 16)
        HD = D // H
        key = jax.random.key(seed)
        ks = jax.random.split(key, 8)
        s = 1.0 / math.sqrt(D)
        x = jax.random.normal(ks[0], (B, N, D), dtype=jnp.float32)
        Wqkv = jax.random.uniform(ks[1], (3 * D, D), jnp.float32, -s, s)
        bqkv = jax.random.uniform(ks[2], (3 * D,), jnp.float32, -s, s)
        Wgate = jax.random.uniform(ks[3], (D, D), jnp.float32, -s, s)
        bgate = jax.random.uniform(ks[4], (D,), jnp.float32, -s, s)
        Wout = jax.random.uniform(ks[5], (D, D), jnp.float32, -s, s)
        bout = jax.random.uniform(ks[6], (D,), jnp.float32, -s, s)
        alphas = jnp.linspace(0.2, 2.0, H)
        deltas = jnp.array([math.log(1.0 + d) for d in OFFSETS], dtype=jnp.float32)
        pos_bias = -deltas[:, None] * alphas[None, :]
        offsets = jnp.array(OFFSETS, dtype=jnp.int32)
        return {'x': x, 'Wqkv': Wqkv, 'bqkv': bqkv, 'Wgate': Wgate, 'bgate': bgate, 'Wout': Wout, 'bout': bout, 'pos_bias': pos_bias, 'offsets': offsets}
    _L1_attn_a_in = _L1_attn_a_setup()

    def _L1_attn_b_setup():
        import jax, jax.numpy as jnp
        import numpy as np
        D_MODEL, N_HEADS, BATCH, SEQ = (128, 16, 2, 256)

        def get_freqs(seq, n_dim):
            inv_freq = 1.0 / 10000.0 ** (jnp.arange(0, n_dim, 2, dtype=jnp.float32) / n_dim)
            pos = jnp.arange(seq, dtype=jnp.float32)
            return pos[:, None] * inv_freq[None, :]

        def rope(x, freq):
            cos = jnp.cos(freq)[None, :, None, :]
            sin = jnp.sin(freq)[None, :, None, :]
            x1, x2 = (x[..., ::2], x[..., 1::2])
            r1 = x1 * cos - x2 * sin
            r2 = x1 * sin + x2 * cos
            return jnp.stack([r1, r2], axis=-1).reshape(x.shape)
        key = jax.random.key(seed)
        ks = jax.random.split(key, 5)
        w_scale = 0.01
        return {'x': jax.random.normal(ks[0], (BATCH, SEQ, D_MODEL), dtype=jnp.float32), 'qw': jax.random.normal(ks[1], (D_MODEL, D_MODEL), dtype=jnp.float32) * w_scale, 'kw': jax.random.normal(ks[2], (D_MODEL, D_MODEL), dtype=jnp.float32) * w_scale, 'vw': jax.random.normal(ks[3], (D_MODEL, D_MODEL), dtype=jnp.float32) * w_scale, 'ow': jax.random.normal(ks[4], (D_MODEL, D_MODEL), dtype=jnp.float32) * w_scale}
    _L1_attn_b_in = _L1_attn_b_setup()

    def _L1_ffn_setup():
        import jax, jax.numpy as jnp
        import numpy as np
        D = 128
        F = 128
        E = 8
        K = 2
        B, T = (2, 256)

        def _moe_forward(x, router_w, w1, w2, shared_gate_up, shared_down, shared_gate_w):
            b, t, d = x.shape
            xf = x.reshape(-1, d)
            n = xf.shape[0]
            logits = xf @ router_w
            probs = jax.nn.softmax(logits, axis=-1)
            topw, topi = jax.lax.top_k(probs, K)
            combine = jnp.zeros((n, E), dtype=probs.dtype).at[jnp.arange(n)[:, None], topi].add(topw)
            h = jax.nn.silu(jnp.einsum('nd,edf->nef', xf, w1))
            ye = jnp.einsum('nef,efd->ned', h, w2)
            routed = jnp.einsum('ne,ned->nd', combine, ye)
            gu = xf @ shared_gate_up
            gate, up = (gu[:, :F], gu[:, F:])
            shared = jax.nn.silu(gate) * up @ shared_down
            shared = jax.nn.sigmoid(xf @ shared_gate_w) * shared
            return (routed + shared).reshape(b, t, d)
        key = jax.random.key(seed)
        ks = jax.random.split(key, 7)
        std = 0.02
        x = jax.random.normal(ks[0], (B, T, D), dtype=jnp.float32)
        router_w = jax.random.normal(ks[1], (D, E), dtype=jnp.float32) * std
        w1 = jax.random.normal(ks[2], (E, D, F), dtype=jnp.float32) * std
        w2 = jax.random.normal(ks[3], (E, F, D), dtype=jnp.float32) * std
        shared_gate_up = jax.random.normal(ks[4], (D, 2 * F), dtype=jnp.float32) * std
        shared_down = jax.random.normal(ks[5], (F, D), dtype=jnp.float32) * std
        shared_gate_w = jax.random.normal(ks[6], (D, 1), dtype=jnp.float32) * std
        return {'x': x, 'router_w': router_w, 'w1': w1, 'w2': w2, 'shared_gate_up': shared_gate_up, 'shared_down': shared_down, 'shared_gate_w': shared_gate_w}
    _L1_ffn_in = _L1_ffn_setup()
    _d = {'L0_attn_a_x': _L0_attn_a_in['x'], 'L0_attn_a_w_qkv': _L0_attn_a_in['w_qkv'], 'L0_attn_a_w_out': _L0_attn_a_in['w_out'], 'L0_attn_a_b_out': _L0_attn_a_in['b_out'], 'L0_attn_b_Wq': _L0_attn_b_in['Wq'], 'L0_attn_b_bq': _L0_attn_b_in['bq'], 'L0_attn_b_Wk': _L0_attn_b_in['Wk'], 'L0_attn_b_bk': _L0_attn_b_in['bk'], 'L0_attn_b_Wv': _L0_attn_b_in['Wv'], 'L0_attn_b_bv': _L0_attn_b_in['bv'], 'L0_attn_b_Wo': _L0_attn_b_in['Wo'], 'L0_attn_b_bo': _L0_attn_b_in['bo'], 'L0_attn_b_decay_params': _L0_attn_b_in['decay_params'], 'L0_attn_b_mix_weights': _L0_attn_b_in['mix_weights'], 'L0_ffn_router_w': _L0_ffn_in['router_w'], 'L0_ffn_w_in': _L0_ffn_in['w_in'], 'L0_ffn_b_in': _L0_ffn_in['b_in'], 'L0_ffn_w_out': _L0_ffn_in['w_out'], 'L0_ffn_b_out': _L0_ffn_in['b_out'], 'L1_attn_a_Wqkv': _L1_attn_a_in['Wqkv'], 'L1_attn_a_bqkv': _L1_attn_a_in['bqkv'], 'L1_attn_a_Wgate': _L1_attn_a_in['Wgate'], 'L1_attn_a_bgate': _L1_attn_a_in['bgate'], 'L1_attn_a_Wout': _L1_attn_a_in['Wout'], 'L1_attn_a_bout': _L1_attn_a_in['bout'], 'L1_attn_a_pos_bias': _L1_attn_a_in['pos_bias'], 'L1_attn_a_offsets': _L1_attn_a_in['offsets'], 'L1_attn_b_qw': _L1_attn_b_in['qw'], 'L1_attn_b_kw': _L1_attn_b_in['kw'], 'L1_attn_b_vw': _L1_attn_b_in['vw'], 'L1_attn_b_ow': _L1_attn_b_in['ow'], 'L1_ffn_router_w': _L1_ffn_in['router_w'], 'L1_ffn_w1': _L1_ffn_in['w1'], 'L1_ffn_w2': _L1_ffn_in['w2'], 'L1_ffn_shared_gate_up': _L1_ffn_in['shared_gate_up'], 'L1_ffn_shared_down': _L1_ffn_in['shared_down'], 'L1_ffn_shared_gate_w': _L1_ffn_in['shared_gate_w']}
    _x0 = _d['L0_attn_a_x']
    _d['L0_attn_a_x'] = jax.random.normal(jax.random.fold_in(jax.random.key(seed), 1), (4, 1024, 128), dtype=_x0.dtype)
    del _x0
    return _d

def reference(L0_attn_a_x, L0_attn_a_w_qkv, L0_attn_a_w_out, L0_attn_a_b_out, L0_attn_b_Wq, L0_attn_b_bq, L0_attn_b_Wk, L0_attn_b_bk, L0_attn_b_Wv, L0_attn_b_bv, L0_attn_b_Wo, L0_attn_b_bo, L0_attn_b_decay_params, L0_attn_b_mix_weights, L0_ffn_router_w, L0_ffn_w_in, L0_ffn_b_in, L0_ffn_w_out, L0_ffn_b_out, L1_attn_a_Wqkv, L1_attn_a_bqkv, L1_attn_a_Wgate, L1_attn_a_bgate, L1_attn_a_Wout, L1_attn_a_bout, L1_attn_a_pos_bias, L1_attn_a_offsets, L1_attn_b_qw, L1_attn_b_kw, L1_attn_b_vw, L1_attn_b_ow, L1_ffn_router_w, L1_ffn_w1, L1_ffn_w2, L1_ffn_shared_gate_up, L1_ffn_shared_down, L1_ffn_shared_gate_w):

    def _L0_attn_a_ref(x, w_qkv, w_out, b_out):
        import jax, jax.numpy as jnp
        import numpy as np
        from math import sqrt
        D_MODEL = 128
        N_HEADS = 16
        B, T, C = x.shape
        H = N_HEADS
        d = C // H
        qkv = x @ w_qkv
        q, k, v = jnp.split(qkv, 3, axis=-1)
        q = q.reshape(B, T, H, d).transpose(0, 2, 1, 3)
        k = k.reshape(B, T, H, d).transpose(0, 2, 1, 3)
        v = v.reshape(B, T, H, d).transpose(0, 2, 1, 3)
        scores = jnp.einsum('bhqd,bhkd->bhqk', q, k) / sqrt(d)
        causal = jnp.tril(jnp.ones((T, T), dtype=bool))
        scores = jnp.where(causal[None, None], scores, -jnp.inf)
        attn = jax.nn.softmax(scores, axis=-1)
        out = jnp.einsum('bhqk,bhkd->bhqd', attn, v)
        out = out.transpose(0, 2, 1, 3).reshape(B, T, C)
        return out @ w_out + b_out

    def _L0_attn_b_ref(x, Wq, bq, Wk, bk, Wv, bv, Wo, bo, decay_params, mix_weights):
        import jax, jax.numpy as jnp
        import numpy as np
        EMBED_DIM = 128
        NUM_HEADS = 16
        HEAD_DIM = EMBED_DIM // NUM_HEADS
        NUM_DECAYS = 2
        BATCH = 2
        SEQ = 256
        W_SCALE = 0.02
        B, S, _ = x.shape
        H, D = (NUM_HEADS, HEAD_DIM)

        def proj(W, b):
            return (jnp.einsum('bse,fe->bsf', x, W) + b).reshape(B, S, H, D).transpose(0, 2, 1, 3)
        q = proj(Wq, bq)
        k = proj(Wk, bk)
        v = proj(Wv, bv)
        attn_scores = jnp.einsum('bhqd,bhkd->bhqk', q, k) / jnp.sqrt(jnp.float32(D))
        t = jnp.arange(S, dtype=jnp.float32)
        time_diffs = jnp.abs(t[:, None] - t[None, :])
        dp = jnp.clip(decay_params, 0.01, 0.9999)
        decay_masks = dp[:, :, None, None] ** time_diffs[None, None, :, :]
        mix = jax.nn.softmax(mix_weights, axis=-1)
        decay_mask = jnp.einsum('hnqk,hn->hqk', decay_masks, mix)
        attn_scores = attn_scores * decay_mask[None]
        attn_probs = jax.nn.softmax(attn_scores, axis=-1)
        out = jnp.einsum('bhqk,bhkd->bhqd', attn_probs, v)
        out = out.transpose(0, 2, 1, 3).reshape(B, S, H * D)
        return jnp.einsum('bse,fe->bsf', out, Wo) + bo

    def _L0_ffn_ref(input_batch, router_w, w_in, b_in, w_out, b_out):
        import jax, jax.numpy as jnp
        import numpy as np
        D, H, E, K = (128, 128, 8, 2)

        def _moe(x, router_w, w_in, b_in, w_out, b_out):
            B, S, Dm = x.shape
            T = B * S
            x2 = x.reshape(T, Dm)
            logits = x2 @ router_w
            probs = jax.nn.softmax(logits, axis=-1)
            top_p, top_e = jax.lax.top_k(probs, K)
            flat_e = top_e.reshape(-1)
            flat_p = top_p.reshape(-1)
            tok = jnp.repeat(jnp.arange(T), K)
            order = jnp.argsort(flat_e)
            se, sp, st = (flat_e[order], flat_p[order], tok[order])
            xd = x2[st]
            N = xd.shape[0]
            h = jnp.zeros((N, H), x.dtype)
            for e in range(E):
                m = (se == e)[:, None]
                h = h + jnp.where(m, jax.nn.gelu(xd @ w_in[e] + b_in[e]), 0.0)
            y = jnp.zeros((N, Dm), x.dtype)
            for e in range(E):
                m = (se == e)[:, None]
                y = y + jnp.where(m, h @ w_out[e] + b_out[e], 0.0)
            y = y * sp[:, None]
            out = jnp.zeros((T, Dm), x.dtype).at[st].add(y)
            return out.reshape(B, S, Dm)
        return _moe(input_batch, router_w, w_in, b_in, w_out, b_out)

    def _L1_attn_a_ref(x, Wqkv, bqkv, Wgate, bgate, Wout, bout, pos_bias, offsets):
        import jax, jax.numpy as jnp
        import numpy as np
        import math
        _DENSE_LOCAL_W = 64
        _DYADIC = [96, 128, 192, 32, 48, 64, 96, 128, 192]
        OFFSETS = sorted(set(range(0, _DENSE_LOCAL_W + 1)) | set(_DYADIC))
        B, N, D, H = (1, 256, 128, 16)
        HD = D // H
        Bx, Nx, Dx = x.shape
        qkv = x @ Wqkv.T + bqkv
        q, k, v = jnp.split(qkv, 3, axis=-1)
        q = q.reshape(Bx, Nx, H, HD).transpose(0, 2, 1, 3)
        k = k.reshape(Bx, Nx, H, HD).transpose(0, 2, 1, 3)
        v = v.reshape(Bx, Nx, H, HD).transpose(0, 2, 1, 3)
        scale = HD ** (-0.5)
        n_idx = jnp.arange(Nx, dtype=jnp.int32)[:, None]
        idx = n_idx - offsets[None, :]
        valid = idx >= 0
        idx_c = jnp.clip(idx, 0, Nx - 1)
        K_all = k[:, :, idx_c, :]
        V_all = v[:, :, idx_c, :]
        scores = jnp.einsum('bhnd,bhnod->bhno', q, K_all) * scale
        scores = scores + pos_bias.T[None, :, None, :]
        scores = jnp.where(valid[None, None], scores, -jnp.inf)
        alpha = jax.nn.softmax(scores, axis=-1)
        out = jnp.einsum('bhno,bhnod->bhnd', alpha, V_all)
        flat = out.transpose(0, 2, 1, 3).reshape(Bx, Nx, Dx)
        gate = jax.nn.sigmoid(x @ Wgate.T + bgate)
        return flat * gate @ Wout.T + bout

    def _L1_attn_b_ref(x, qw, kw, vw, ow):
        import jax, jax.numpy as jnp
        import numpy as np
        D_MODEL, N_HEADS, BATCH, SEQ = (128, 16, 2, 256)

        def get_freqs(seq, n_dim):
            inv_freq = 1.0 / 10000.0 ** (jnp.arange(0, n_dim, 2, dtype=jnp.float32) / n_dim)
            pos = jnp.arange(seq, dtype=jnp.float32)
            return pos[:, None] * inv_freq[None, :]

        def rope(x, freq):
            cos = jnp.cos(freq)[None, :, None, :]
            sin = jnp.sin(freq)[None, :, None, :]
            x1, x2 = (x[..., ::2], x[..., 1::2])
            r1 = x1 * cos - x2 * sin
            r2 = x1 * sin + x2 * cos
            return jnp.stack([r1, r2], axis=-1).reshape(x.shape)
        batch, seq, dim = x.shape
        n_heads = N_HEADS
        n_dim = dim // n_heads
        Q = (x @ qw).astype(jnp.float32).reshape(batch, seq, n_heads, n_dim)
        K = (x @ kw).astype(jnp.float32).reshape(batch, seq, n_heads, n_dim)
        V = (x @ vw).astype(jnp.float32).reshape(batch, seq, n_heads, n_dim)
        freq = get_freqs(seq, n_dim)
        Q = rope(Q, freq)
        K = rope(K, freq)
        Q = jnp.transpose(Q, (0, 2, 1, 3))
        K = jnp.transpose(K, (0, 2, 1, 3))
        V = jnp.transpose(V, (0, 2, 1, 3))
        scale = jnp.sqrt(jnp.float32(n_dim))
        score = jnp.einsum('bhqd,bhkd->bhqk', Q, K) / scale
        causal = jnp.tril(jnp.ones((1, 1, seq, seq), dtype=jnp.float32))
        score = score - 10000000000.0 * (1.0 - causal)
        score = score - jnp.max(score, axis=-1, keepdims=True)
        weights = jax.nn.softmax(score, axis=-1)
        attn = jnp.einsum('bhqk,bhkd->bhqd', weights, V)
        merged = jnp.transpose(attn, (0, 2, 1, 3)).reshape(batch, seq, dim)
        return (merged @ ow).astype(x.dtype)

    def _L1_ffn_ref(x, router_w, w1, w2, shared_gate_up, shared_down, shared_gate_w):
        import jax, jax.numpy as jnp
        import numpy as np
        D = 128
        F = 128
        E = 8
        K = 2
        B, T = (2, 256)

        def _moe_forward(x, router_w, w1, w2, shared_gate_up, shared_down, shared_gate_w):
            b, t, d = x.shape
            xf = x.reshape(-1, d)
            n = xf.shape[0]
            logits = xf @ router_w
            probs = jax.nn.softmax(logits, axis=-1)
            topw, topi = jax.lax.top_k(probs, K)
            combine = jnp.zeros((n, E), dtype=probs.dtype).at[jnp.arange(n)[:, None], topi].add(topw)
            h = jax.nn.silu(jnp.einsum('nd,edf->nef', xf, w1))
            ye = jnp.einsum('nef,efd->ned', h, w2)
            routed = jnp.einsum('ne,ned->nd', combine, ye)
            gu = xf @ shared_gate_up
            gate, up = (gu[:, :F], gu[:, F:])
            shared = jax.nn.silu(gate) * up @ shared_down
            shared = jax.nn.sigmoid(xf @ shared_gate_w) * shared
            return (routed + shared).reshape(b, t, d)
        return _moe_forward(x, router_w, w1, w2, shared_gate_up, shared_down, shared_gate_w)
    x = L0_attn_a_x
    x = x + _L0_attn_a_ref(_layernorm(x, axis=-1), L0_attn_a_w_qkv, L0_attn_a_w_out, L0_attn_a_b_out)
    x = x + _L0_ffn_ref(_layernorm(x, axis=-1), L0_ffn_router_w, L0_ffn_w_in, L0_ffn_b_in, L0_ffn_w_out, L0_ffn_b_out)
    x = x + _L0_attn_b_ref(_layernorm(x, axis=-1), L0_attn_b_Wq, L0_attn_b_bq, L0_attn_b_Wk, L0_attn_b_bk, L0_attn_b_Wv, L0_attn_b_bv, L0_attn_b_Wo, L0_attn_b_bo, L0_attn_b_decay_params, L0_attn_b_mix_weights)
    x = x + _L0_ffn_ref(_layernorm(x, axis=-1), L0_ffn_router_w, L0_ffn_w_in, L0_ffn_b_in, L0_ffn_w_out, L0_ffn_b_out)
    x = x + _L1_attn_a_ref(_layernorm(x, axis=-1), L1_attn_a_Wqkv, L1_attn_a_bqkv, L1_attn_a_Wgate, L1_attn_a_bgate, L1_attn_a_Wout, L1_attn_a_bout, L1_attn_a_pos_bias, L1_attn_a_offsets)
    x = x + _L1_ffn_ref(_layernorm(x, axis=-1), L1_ffn_router_w, L1_ffn_w1, L1_ffn_w2, L1_ffn_shared_gate_up, L1_ffn_shared_down, L1_ffn_shared_gate_w)
    x = x + _L1_attn_b_ref(_layernorm(x, axis=-1), L1_attn_b_qw, L1_attn_b_kw, L1_attn_b_vw, L1_attn_b_ow)
    x = x + _L1_ffn_ref(_layernorm(x, axis=-1), L1_ffn_router_w, L1_ffn_w1, L1_ffn_w2, L1_ffn_shared_gate_up, L1_ffn_shared_down, L1_ffn_shared_gate_w)
    return x

_drawn_inputs = setup_inputs


def setup_inputs(seed=0):
    import zlib

    import numpy as np

    out = dict(_drawn_inputs(seed))
    spreads = {'L0_attn_a_b_out': (0.0, 0.1),
     'L0_attn_b_bq': (0.0, 0.8),
     'L0_attn_b_bk': (0.0, 2.0),
     'L0_attn_b_bv': (0.0, 0.1),
     'L0_attn_b_bo': (0.0, 0.1),
     'L0_ffn_b_in': (0.0, 0.1),
     'L0_ffn_b_out': (0.0, 0.1)}
    factors = {'L0_attn_b_Wq': 8.0,
     'L0_attn_b_Wk': 8.0,
     'L0_attn_b_Wv': 5.788,
     'L0_attn_b_decay_params': 8.0,
     'L0_attn_b_mix_weights': 8.0,
     'L1_attn_a_bqkv': 4.132,
     'L1_attn_a_Wgate': 3.403,
     'L1_attn_a_bgate': 23.133,
     'L1_attn_b_qw': 8.0,
     'L1_attn_b_kw': 8.0,
     'L1_attn_b_vw': 8.0,
     'L1_attn_b_ow': 8.0,
     'L1_ffn_router_w': 6.505,
     'L1_ffn_w1': 5.648,
     'L1_ffn_w2': 5.611,
     'L1_ffn_shared_gate_up': 8.0,
     'L1_ffn_shared_down': 8.0,
     'L1_ffn_shared_gate_w': 8.0}
    for name, (base, spread) in spreads.items():
        noise = np.random.default_rng([zlib.crc32(name.encode()), seed]).standard_normal(out[name].shape)
        drawn = base * np.exp(spread * noise) if base else spread * noise
        out[name] = jnp.asarray(drawn.astype(out[name].dtype))
    for name, factor in factors.items():
        out[name] = (out[name] * factor).astype(out[name].dtype)
    return out
```

```python
import concourse.bass as bass
from concourse import mybir
from contextlib import ExitStack

fp32 = mybir.dt.float32
bf16 = mybir.dt.bfloat16
i32 = mybir.dt.int32
ALU = mybir.AluOpType
ACT = mybir.ActivationFunctionType
AX = mybir.AxisListType

B, T, D = 4, 1024, 128
H, HD = 16, 8
E = 8
P = 128
TILES = B * T // P
TPB = T // P
CH = 512
TPC = CH // P
NCH = B * T // CH
G, GH = 4, 4
PARTS = 3
ROWS = PARTS * PARTS * HD
VW = HD + 1
NEG = -1.0e30
SCALE = float(HD) ** -0.5
EPS = 1e-5
LN_D = 32
NOFF = 68
TABX = 1920
ROWX = TABX + 127


class Signal:

    def __init__(self, sem):
        self.sem, self.base = sem, 1

    def __call__(self, n):
        return self.sem, self.base + n

    def close(self, total):
        self.base += total


def hybrid_program(nc, t, out):
    ctx = ExitStack()
    with ctx:
        used = {}

        def sb(name, shape, dt=fp32, where=ctx):
            used[name] = used.get(name, 0) + 1
            name += f"_{used[name]}" if used[name] > 1 else ""
            return where.enter_context(nc.sbuf_tensor(name, shape, dt))

        def dram(name, shape, dt=fp32):
            return nc.dram_tensor(name, shape, dt, kind="Internal").ap()

        signals = {}

        def sig(name):
            if name not in signals:
                signals[name] = Signal(ctx.enter_context(nc.semaphore(name)))
                nc.sync.sem_inc(signals[name].sem, 1)
            return signals[name]

        x_sb = sb("x_sb", [P, TILES + TPC, D])
        stats = sb("stats", [P, TILES, 6])
        meanvar = sb("meanvar", [P, TILES + TPC, 2])
        rstd = sb("rstd", [P, TILES + TPC])
        ident = sb("ident", [P, P])
        eps = sb("eps", [P, 1])
        xn = sb("xn", [P, 2, TPC, D])
        xTc = sb("xTc", [P, 2, CH])
        V_sb = sb("V_sb", [P, B, G, TPB, GH * VW])
        bank = [ctx.enter_context(nc.psum_tensor(f"bank{i}", [P, CH], fp32)) for i in range(8)]

        q3_d = dram("q3_d", [G * B, PARTS, LN_D * T], bf16)
        k3_d = dram("k3_d", [G * B, PARTS, LN_D * T], bf16)
        ol_d = dram("ol_d", [G * B * GH, VW, T])
        rl_d = dram("rl_d", [G * B * GH, T])
        decay_d = dram("decay_d", [H, ROWX])
        bias_d = dram("bias_d", [H, T + 127])
        biasr_d = dram("biasr_d", [H, T + 127])
        decay_t = dram("decay_t", [H, P, TABX])
        bias_t = dram("bias_t", [H, P, T])
        biasr_t = dram("biasr_t", [H, P, T])
        tables_made = sig("tables_made")

        def at(ap, offset, dims):
            return bass.AP(ap.tensor, offset, dims)

        def prologue():
            W = T + 127
            with ExitStack() as mem:
                mixes = sb("mixes", [H, 2], where=mem)
                clip = sb("clip", [H, 2], where=mem)
                lndp = sb("lndp", [H, 2], where=mem)
                mix_nmax = sb("mix_nmax", [H, 1], where=mem)
                mix_exp = sb("mix_exp", [H, 2], where=mem)
                mix_sum = sb("mix_sum", [H, 2], where=mem)
                mix = sb("mix", [H, 2], where=mem)
                dist = sb("dist", [H, ROWX], where=mem)
                power = sb("power", [H, 2, ROWX], where=mem)
                decay_row = sb("decay_row", [H, ROWX], where=mem)
                off_i = sb("off_i", [NOFF, 1], i32, where=mem)
                off_f = sb("off_f", [NOFF, 1], where=mem)
                pbT = sb("pbT", [H, NOFF], where=mem)
                pb_nmax = sb("pb_nmax", [H, 1], where=mem)
                pexp = sb("pexp", [H, NOFF], where=mem)
                three = sb("three", [NOFF, 96], where=mem)
                deltas = sb("deltas", [NOFF, 2, W], where=mem)
                hot = sb("hot", [NOFF, 2, W], where=mem)
                count = sb("count", [H, 2, W], where=mem)
                single = sb("single", [H, 2, W], where=mem)
                esum = sb("esum", [H, 2, W], where=mem)
                lse = sb("lse", [H, 2, W], where=mem)
                flag = sb("flag", [H, 2, W], where=mem)
                row = sb("row", [H, 2, W], where=mem)
                loaded, filled, three_set = sig("pro_loaded"), sig("pro_filled"), sig("pro_three_set")
                vstep = sig("pro_vstep")
                logs, mixexp, powers, pbexp, lse_done = (sig("pro_logs"), sig("pro_mixexp"), sig("pro_powers"),
                                                         sig("pro_pbexp"), sig("pro_lse"))
                pexpT, sums, stored = sig("pro_pexpT"), sig("pro_sums"), sig("pro_stored")
                clipped, mixed, decays_ready, biasmax, hot_ready, esum_ready, rows_ready = (
                    sig(n) for n in ("pro_clipped", "pro_mixed", "pro_decays", "pro_biasmax", "pro_hot",
                                     "pro_esum", "pro_rows"))
                block = mem.enter_context(nc.Block())
                LOADS = 10
                cuts = [(a, min(a + CH, W)) for a in range(0, W, CH)]

                @block.sync
                def _(sp):
                    for dst, src in ((x_sb[:, 0:TILES, :], t["x"].rearrange("(n p) f -> p n f", p=P)),
                                     (ident[:], t["ident"]), (clip[:], t["decay"]), (mixes[:], t["mix"]),
                                     (dist[:], t["dist"].partition_broadcast(H)), (off_i[:], t["offsets"]),
                                     (pbT[:], t["pos_biasT"]), (three[:, 32:32 + H], t["pos_bias"]),
                                     (deltas[:, 0, :], t["delta"].partition_broadcast(NOFF)),
                                     (deltas[:, 1, :], t["deltar"].partition_broadcast(NOFF))):
                        if dst.tensor.name == three.name:
                            sp.wait_ge(*three_set(1))
                        sp.dma_start(dst, src).then_inc(loaded.sem, 16)
                    sp.wait_ge(*decays_ready(1))
                    sp.dma_start(decay_d, decay_row[:]).then_inc(stored.sem, 16)
                    sp.wait_ge(*rows_ready(1))
                    sp.dma_start(bias_d, row[:, 0, :]).then_inc(stored.sem, 16)
                    sp.dma_start(biasr_d, row[:, 1, :]).then_inc(stored.sem, 16)
                    sp.wait_ge(*stored(48))
                    for dst, src, width in ((decay_t, decay_d, TABX), (biasr_t, biasr_d, T), (bias_t, bias_d, T)):
                        sp.dma_start(dst, at(src, 127, [[width + 127, H], [-1, P], [1, width]])).then_inc(tables_made.sem, 16)

                @block.gpsimd
                def _(pool):
                    nc.gpsimd.memset(three[:], 1.0).then_inc(three_set.sem, 1)
                    nc.gpsimd.memset(V_sb[:], 1.0).then_inc(filled.sem, 1)
                    nc.gpsimd.memset(x_sb[:, TILES:TILES + TPC, :], 0.0).then_inc(filled.sem, 1)
                    nc.gpsimd.memset(meanvar[:, TILES:TILES + TPC, :], 0.0).then_inc(filled.sem, 1)
                    nc.gpsimd.memset(rstd[:, TILES:TILES + TPC], 1.0).then_inc(filled.sem, 1)
                    nc.gpsimd.memset(eps[:], EPS).then_inc(filled.sem, 1)

                @block.vector
                def _(v):
                    done = [0]

                    def step(ins):
                        done[0] += 1
                        ins.then_inc(vstep.sem, 1)
                        v.wait_ge(*vstep(done[0]))

                    v.wait_ge(*loaded(16 * LOADS))
                    step(nc.vector.tensor_scalar(clip[:], clip[:], 0.01, 0.9999, ALU.max, ALU.min))
                    nc.vector.tensor_reduce(mix_nmax[:], mixes[:], AX.X, ALU.max, negate=True).then_inc(clipped.sem, 1)
                    nc.vector.tensor_reduce(pb_nmax[:], pbT[:], AX.X, ALU.max, negate=True).then_inc(biasmax.sem, 1)
                    step(nc.vector.tensor_copy(off_f[:], off_i[:]))
                    nc.vector.tensor_scalar(hot[:, :, :], deltas[:, :, :], off_f[:, 0:1], None,
                                            ALU.is_equal).then_inc(hot_ready.sem, 1)
                    v.wait_ge(*pexpT(1))
                    nc.vector.tensor_copy(three[:, 64:64 + H], bank[7][0:NOFF, 0:H]).then_inc(hot_ready.sem, 1)
                    v.wait_ge(*mixexp(1))
                    step(nc.vector.reduce_sum(mix_sum[:, 0:1], mix_exp[:], AX.X))
                    step(nc.vector.reciprocal(mix_sum[:, 1:2], mix_sum[:, 0:1]))
                    step(nc.vector.tensor_scalar(mix[:], mix_exp[:], mix_sum[:, 1:2], None, ALU.mult))
                    v.wait_ge(*powers(2))
                    step(nc.vector.tensor_scalar(decay_row[:], power[:, 1, :], mix[:, 1:2], None, ALU.mult))
                    nc.vector.scalar_tensor_tensor(out=decay_row[:], in0=power[:, 0, :], scalar=mix[:, 0:1],
                                                   in1=decay_row[:], op0=ALU.mult,
                                                   op1=ALU.add).then_inc(decays_ready.sem, 1)
                    for r in range(2):
                        for c, (a, b) in enumerate(cuts):
                            k = r * len(cuts) + c
                            v.wait_ge(*sums(k + 1))
                            nc.vector.tensor_copy(count[:, r, a:b], bank[k][0:H, 0:b - a])
                            nc.vector.tensor_copy(single[:, r, a:b], bank[k][32:32 + H, 0:b - a])
                            step(nc.vector.tensor_scalar(esum[:, r, a:b], bank[k][64:64 + H, 0:b - a],
                                                         1e-18, None, ALU.max))
                    nc.vector.tensor_scalar(flag[:], count[:], 1.5, None, ALU.is_gt).then_inc(esum_ready.sem, 1)
                    v.wait_ge(*lse_done(1))
                    step(nc.vector.tensor_scalar(lse[:], lse[:], pb_nmax[:, 0:1], None, ALU.subtract))
                    step(nc.vector.tensor_tensor(lse[:], lse[:], single[:], ALU.subtract))
                    step(nc.vector.tensor_tensor(lse[:], lse[:], flag[:], ALU.mult))
                    step(nc.vector.tensor_tensor(lse[:], lse[:], single[:], ALU.add))
                    step(nc.vector.tensor_scalar(flag[:], count[:], 0.5, NEG, ALU.is_lt, ALU.mult))
                    nc.vector.tensor_tensor(row[:], lse[:], flag[:], ALU.add).then_inc(rows_ready.sem, 1)

                @block.scalar
                def _(act):
                    act.wait_ge(*clipped(1))
                    nc.scalar.activation(lndp[:], clip[:], ACT.Ln).then_inc(logs.sem, 1)
                    nc.scalar.activation(mix_exp[:], mixes[:], ACT.Exp, bias=mix_nmax[:, 0:1]).then_inc(mixexp.sem, 1)
                    act.wait_ge(*biasmax(1))
                    nc.scalar.activation(pexp[:], pbT[:], ACT.Exp, bias=pb_nmax[:, 0:1]).then_inc(pbexp.sem, 1)
                    act.wait_ge(*logs(1))
                    for n in range(2):
                        nc.scalar.activation(power[:, n, :], dist[:], ACT.Exp, scale=lndp[:, n:n + 1]).then_inc(powers.sem, 1)
                    act.wait_ge(*esum_ready(1))
                    nc.scalar.activation(lse[:], esum[:], ACT.Ln).then_inc(lse_done.sem, 1)

                @block.tensor
                def _(pe):
                    pe.wait_ge(*loaded(16 * LOADS))
                    pe.wait_ge(*pbexp(1))
                    nc.tensor.transpose(bank[7][0:NOFF, 0:H], pexp[:], ident[0:H, 0:H]).then_inc(pexpT.sem, 1)
                    pe.wait_ge(*hot_ready(2))
                    for r in range(2):
                        for c, (a, b) in enumerate(cuts):
                            nc.tensor.matmul(bank[r * len(cuts) + c][0:96, 0:b - a], three[:], hot[:, r, a:b],
                                             start=True, stop=True).then_inc(sums.sem, 1)

        def norm_signals():
            return {n: sig("ln_" + n) for n in ("stats", "aggr", "std", "rstd", "norm", "transposed", "copied")}

        def close_norm(s):
            for n, total in (("stats", TILES // TPC), ("aggr", 1), ("std", 1), ("rstd", 1),
                             ("norm", NCH + 1), ("transposed", NCH + 1), ("copied", NCH + 1)):
                s[n].close(total)

        def vector_statistics(v, s):
            with v.Fori(0, TILES // TPC) as c:
                for k in range(TPC):
                    ins = nc.vector.bn_stats(stats[:, bass.ds(c * TPC + k, 1), :], x_sb[:, bass.ds(c * TPC + k, 1), :])
                ins.then_inc(s["stats"].sem, 1)
            v.wait_ge(*s["stats"](TILES // TPC))
            for n in range(TILES):
                ins = nc.vector.bn_aggr(meanvar[:, n, :], stats[:, n, :])
            ins.then_inc(s["aggr"].sem, 1)
            v.wait_ge(*s["std"](1))
            nc.vector.reciprocal(rstd[:, 0:TILES], rstd[:, 0:TILES]).then_inc(s["rstd"].sem, 1)
            v.wait_ge(*s["rstd"](1))

        def scalar_statistics(act, s):
            act.wait_ge(*s["aggr"](1))
            nc.scalar.activation(rstd[:, 0:TILES], meanvar[:, 0:TILES, 1], ACT.Sqrt,
                                 bias=eps[:, 0:1]).then_inc(s["std"].sem, 1)

        def vector_normalise(v, s, c, slot):
            v.wait_ge(*s["transposed"](c - 1 if not isinstance(c, int) or c > 1 else 0))
            for k in range(TPC):
                tile = c * TPC + k
                ins = nc.vector.tensor_scalar(
                    xn[:, slot, k, :], x_sb[:, tile, :] if isinstance(c, int) else x_sb[:, bass.ds(tile, 1), :],
                    meanvar[:, tile, 0:1] if isinstance(c, int) else meanvar[:, bass.ds(tile, 1), 0],
                    rstd[:, tile:tile + 1] if isinstance(c, int) else rstd[:, bass.ds(tile, 1)],
                    ALU.subtract, ALU.mult)
            ins.then_inc(s["norm"].sem, 1)

        def tensor_transpose(pe, s, c, slot):
            pe.wait_ge(*s["norm"](c + 1))
            pe.wait_ge(*s["copied"](c))
            for k in range(TPC):
                ins = nc.tensor.transpose(bank[0][:, k * P:(k + 1) * P], xn[:, slot, k, :], ident[:])
            ins.then_inc(s["transposed"].sem, 1)

        def project(cfg):
            rope, biased, gated = cfg["rope"], cfg["biased"], cfg["gated"]
            NQ = 4 if rope else 2
            with ExitStack() as mem:
                w = sb("w", [P, cfg["nw"], P], where=mem)
                b_qk = sb("b_qk", [P, 3], where=mem)
                b_q = sb("b_q", [P, 1], where=mem)
                b_v = sb("b_v", [P, P], where=mem)
                turn = sb("turn", [P, 4, T], where=mem) if rope else None
                full = sb("full", [P, 2, CH], where=mem)
                direct = sb("direct", [P, 2, CH], where=mem) if rope else None
                partner = sb("partner", [P, 2, CH], where=mem) if rope else None
                rest = sb("rest", [P, 2, 2, CH], where=mem)
                split = sb("split", [P, 2, 2, PARTS, CH], bf16, where=mem)
                ln = norm_signals()
                loaded, scaled = sig("pj_loaded"), sig("pj_bias_scaled")
                made = [sig(f"pj_product{i}") for i in range(NQ)]
                v_made, g_made = sig("pj_v_product"), sig("pj_gate_product")
                v_out, g_out = sig("pj_v_copied"), sig("pj_gate_done")
                turned = sig("pj_turned")
                f_ready, hi_ready = sig("pj_float_ready"), sig("pj_high_ready")
                r_ready, mid_ready, lo_ready = sig("pj_rest_ready"), sig("pj_middle_ready"), sig("pj_low_ready")
                stored = [sig("pj_stored0"), sig("pj_stored1")]
                def v_slot(b, half, k):
                    flat = V_sb[:, :, :, :, :].rearrange("p b g n c -> p b (g n c)")
                    tile = flat[:, bass.ds(b, 1), :].rearrange("p b (g n h d) -> p b g n h d", g=G, n=TPB, h=GH)
                    return tile[:, 0, :, half * TPC + k, :, 0:HD]

                block = mem.enter_context(nc.Block())
                nloads = 1 + 2 * biased + rope

                @block.sync
                def _(sp):
                    sp.dma_start(w[:], cfg["w"].rearrange("p (n f) -> p n f", f=P)).then_inc(loaded.sem, 16)
                    if biased:
                        sp.dma_start(b_qk[:], cfg["b_qk"]).then_inc(loaded.sem, 16)
                        sp.dma_start(b_v[:], cfg["b_v"].partition_broadcast(P)).then_inc(loaded.sem, 16)
                    if rope:
                        sp.dma_start(turn[:], t["turn"].rearrange("p (n f) -> p n f", f=T)).then_inc(loaded.sem, 16)
                    with sp.Fori(0, B) as b:
                        for half in range(2):
                            for n, dst in enumerate((q3_d, k3_d)):
                                sp.wait_ge(*lo_ready(4 * b + 2 * half + n + 1))
                                for g in range(G):
                                    sp.dma_start(
                                        at(dst, b * (PARTS * LN_D * T) + (g * B * PARTS * LN_D * T + half * CH),
                                           [[T, LN_D], [LN_D * T, PARTS], [1, CH]]),
                                        split[LN_D * g:LN_D * (g + 1), half, n, :, :]).then_inc(stored[half].sem, 16)
                    for half in range(2):
                        sp.wait_ge(*stored[half](16 * 2 * G * B))

                @block.tensor
                def _(pe):
                    pe.wait_ge(*loaded(16 * nloads))
                    tensor_transpose(pe, ln, 0, 0)
                    with pe.Fori(0, B) as b:
                        for half in range(2):
                            c = b * 2 + half
                            tensor_transpose(pe, ln, c + 1, 1 - half)
                            pe.wait_ge(*ln["copied"](c + 1))
                            for i in range(NQ):
                                if rope:
                                    pe.wait_ge(*turned(2 * c))
                                else:
                                    pe.wait_ge(*f_ready(2 * c))
                                nc.tensor.matmul(bank[1 + i][:], w[:, i, :], xTc[:, half, :], start=True,
                                                 stop=True).then_inc(made[i].sem, 1)
                            pe.wait_ge(*v_out(c))
                            for k in range(TPC):
                                ins = nc.tensor.matmul(bank[5][:, k * P:(k + 1) * P], xTc[:, half, k * P:(k + 1) * P],
                                                       w[:, NQ, :], start=True, stop=True)
                            ins.then_inc(v_made.sem, 1)
                            if gated:
                                pe.wait_ge(*g_out(c))
                                nc.tensor.matmul(bank[6][:], w[:, NQ + 1, :], xTc[:, half, :], start=True,
                                                 stop=True).then_inc(g_made.sem, 1)

                @block.scalar
                def _(act):
                    scalar_statistics(act, ln)

                    def copy_transposed(c, slot):
                        act.wait_ge(*ln["transposed"](c + 1))
                        if not isinstance(c, int):
                            act.wait_ge(*(g_made if gated else v_made)(c - 1))
                        nc.scalar.activation(xTc[:, slot, :], bank[0][:], ACT.Copy).then_inc(ln["copied"].sem, 1)

                    act.wait_ge(*loaded(16 * nloads))
                    if biased:
                        act.wait_ge(*scaled(1))
                    copy_transposed(0, 0)
                    with act.Fori(0, B) as b:
                        for half in range(2):
                            c = b * 2 + half
                            copy_transposed(c + 1, 1 - half)
                            for n in range(2):
                                m = 2 * c + n
                                if not rope:
                                    act.wait_ge(*made[n](c + 1))
                                    act.wait_ge(*r_ready(2 * c))
                                    if biased:
                                        ins = nc.scalar.activation(full[:, n, :], bank[1 + n][:], ACT.Identity,
                                                                   bias=(b_q[:, 0:1], b_qk[:, 1:2])[n],
                                                                   scale=(SCALE, 1.0)[n])
                                    else:
                                        ins = nc.scalar.activation(full[:, n, :], bank[1 + n][:], ACT.Copy,
                                                                   scale=(SCALE, 1.0)[n])
                                    ins.then_inc(f_ready.sem, 1)
                                act.wait_ge(*f_ready(m + 1))
                                act.wait_ge(*stored[half](b * (16 * 2 * G)))
                                nc.scalar.activation(split[:, half, n, 0, :], full[:, n, :], ACT.Copy).then_inc(hi_ready.sem, 1)
                            if not biased:
                                act.wait_ge(*v_made(c + 1))
                                for k in range(TPC):
                                    ins = nc.scalar.activation(v_slot(b, half, k),
                                                               bank[5][:, k * P:(k + 1) * P].rearrange("p (g h d) -> p g h d", g=G, h=GH), ACT.Copy)
                                ins.then_inc(v_out.sem, 1)
                            if gated:
                                act.wait_ge(*g_made(c + 1))
                                nc.scalar.activation(gate_sb[0][:, bass.ds(c * CH, CH)], bank[6][:], ACT.Sigmoid,
                                                     bias=b_qk[:, 2:3]).then_inc(g_out.sem, 1)

                @block.vector
                def _(v):
                    v.wait_ge(*loaded(16 * nloads))
                    if biased:
                        nc.vector.tensor_scalar(b_q[:], b_qk[:, 0:1], SCALE, None, ALU.mult).then_inc(scaled.sem, 1)
                    vector_statistics(v, ln)
                    vector_normalise(v, ln, 0, 0)
                    with v.Fori(0, B) as b:
                        for half in range(2):
                            c = b * 2 + half
                            vector_normalise(v, ln, c + 1, 1 - half)
                            if rope:
                                for n in range(2):
                                    v.wait_ge(*f_ready(2 * c))
                                    for i, dst in ((n, direct), (n + 2, partner)):
                                        v.wait_ge(*made[i](c + 1))
                                        ins = nc.vector.tensor_tensor(dst[:, n, :], bank[1 + i][:],
                                                                      turn[:, i, half * CH:(half + 1) * CH], ALU.mult)
                                    ins.then_inc(turned.sem, 1)
                            if biased:
                                v.wait_ge(*v_made(c + 1))
                                for k in range(TPC):
                                    ins = nc.vector.tensor_tensor(v_slot(b, half, k),
                                                                  bank[5][:, k * P:(k + 1) * P].rearrange("p (g h d) -> p g h d", g=G, h=GH),
                                                                  b_v[:, :].rearrange("p (g h d) -> p g h d", g=G, h=GH), ALU.add)
                                ins.then_inc(v_out.sem, 1)
                            for n in range(2):
                                m = 2 * c + n
                                v.wait_ge(*hi_ready(m + 1))
                                nc.vector.tensor_tensor(rest[:, n, 0, :], full[:, n, :], split[:, half, n, 0, :],
                                                        ALU.subtract).then_inc(r_ready.sem, 1)
                                v.wait_ge(*r_ready(m + 1))
                                nc.vector.tensor_copy(split[:, half, n, 1, :], rest[:, n, 0, :]).then_inc(mid_ready.sem, 1)
                                v.wait_ge(*mid_ready(m + 1))
                                nc.vector.tensor_tensor(split[:, half, n, 2, :], rest[:, n, 0, :], split[:, half, n, 1, :],
                                                        ALU.subtract).then_inc(lo_ready.sem, 1)

                if rope:
                    @block.gpsimd
                    def _(pool):
                        with pool.Fori(0, B) as b:
                            for half in range(2):
                                c = b * 2 + half
                                for n in range(2):
                                    pool.wait_ge(*turned(2 * c + n + 1))
                                    pool.wait_ge(*r_ready(2 * c))
                                    nc.gpsimd.tensor_tensor(full[:, n, :], direct[:, n, :], partner[:, n, :],
                                                            ALU.add).then_inc(f_ready.sem, 1)

            close_norm(ln)
            for s, n in ((loaded, 16 * nloads), (scaled, int(biased)), (v_made, NCH), (g_made, NCH * gated),
                         (v_out, NCH), (g_out, NCH * gated), (turned, 2 * NCH * rope), (f_ready, 2 * NCH),
                         (hi_ready, 2 * NCH), (r_ready, 2 * NCH), (mid_ready, 2 * NCH), (lo_ready, 2 * NCH),
                         (stored[0], 16 * 2 * G * B), (stored[1], 16 * 2 * G * B)):
                s.close(n)
            for s in made:
                s.close(NCH)

        def attend(cfg):
            kind = cfg["kind"]
            full = kind == "decay"
            adds = kind == "sparse"
            STEPS = G * B
            def key_tiles(I):
                if full:
                    return list(range(TPB))
                return [0] + [j for j in range(TPC * I, TPC * (I + 1)) if j] + list(range(1, TPC * I))

            units = [(I, j, 0 if full else max(0, P * j - CH * I)) for I in range(T // CH) for j in key_tiles(I)]
            U = len(units)
            chunk_end = [u == U - 1 or units[u + 1][0] != units[u][0] for u in range(U)]
            diagonal = [] if kind != "causal" else [u for u, (I, j, q0) in enumerate(units) if j >= TPC * I]
            parts = [(h, i, m, min(CH, (T if full else P * (i + 1)) - CH * m))
                     for i in range(TPB) for h in range(GH) for m in range(T // CH) if full or P * (i + 1) > CH * m]
            NP = len(parts)
            UM = U - 2
            wide = [CH - q0 for I, j, q0 in units[:UM] for h in range(GH)]
            slot_end, n = [], 0
            for k in range(len(wide)):
                due = sum(wide[:k + 1]) * sum(p[3] for p in parts) / sum(wide)
                while n < NP and sum(p[3] for p in parts[:n + 1]) <= due + 1e-6:
                    n += 1
                slot_end.append(n)
            assert n == NP

            def slot(u, h):
                k = u * GH + h
                return range(slot_end[k - 1] if k else 0, slot_end[k]) if u < UM else range(0)

            MW = TABX if full else T
            with ExitStack() as mem:
                QA = [sb(f"QA{i}", [ROWS + 1, GH, T], bf16, where=mem) for i in range(B)]
                KA = [sb(f"KA{i}", [ROWS + 1, GH, T], bf16, where=mem) for i in range(B)]
                Vt = [sb(f"Vt{i}", [P, TPB, GH * VW], where=mem) for i in range(B)]
                Ex = sb("Ex", [P, 2, GH, CH], where=mem)
                Ov = sb("Ov", [P, T // CH, CH], where=mem)
                mx = sb("mx", [P, GH * TPB, 2], where=mem)
                nmax = sb("nmax", [P, GH * TPB], where=mem)
                nrow = sb("nrow", [GH * TPB, P], bf16, where=mem)
                waste = sb("waste", [P, 2, CH], bf16, where=mem)
                ntab = GH if kind != "causal" else 1
                tab_f = sb("tab_f", [P, 1, MW], where=mem) if kind != "causal" else None
                tab_m = sb("tab_m", [P, ntab, MW], bf16, where=mem)
                tab_e = sb("tab_e", [P, GH, MW], where=mem) if kind != "causal" else None
                pick = sb("pick", [ROWS + 1, P], bf16, where=mem) if full else None

                ready = [sig(f"at_operands{i}") for i in range(B)]
                once = sig("at_constants")
                filled = sig("at_filled")
                tabf, tabm, tabe = sig("at_row_table"), sig("at_max_table"), sig("at_exp_table")
                m_scores, m_taken = sig("at_first_scores"), sig("at_maxima")
                m_seen, d_seen = sig("at_first_scores_seen"), sig("at_diagonal_seen")
                n_ready, n_turned, n_copied, n_stored = (sig("at_negated"), sig("at_negated_turned"),
                                                         sig("at_negated_copied"), sig("at_negated_stored"))
                scores, biased, lowered, exped, masked = (sig("at_scores"), sig("at_scores_biased"),
                                                          sig("at_scores_lowered"), sig("at_exp"), sig("at_masked"))
                summed, o_out, o_stored = sig("at_values_summed"), sig("at_output_copied"), [sig("at_output_stored0"), sig("at_output_stored1")]
                block = mem.enter_context(nc.Block())
                NLOAD = 2 + PARTS
                NONCE = B + (kind == "causal") + full
                S_BANKS, M_BANKS, O_BANK = (0, 1, 2, 3), (4, 5, 6), 7

                def step_of(g, b):
                    return g * B + b

                def over_steps(eng, body):
                    with eng.Fori(0, G - 1) as g:
                        for b in range(B):
                            body(g, b, False)
                    for b in range(B):
                        body(G - 1, b, b == B - 1)

                @block.sync
                def _(sp):
                    def load(g, b):
                        it = step_of(g, b)
                        base = it * (PARTS * LN_D * T)
                        sp.dma_start(QA[b][0:ROWS, :, :], at(q3_d, base, [[0, PARTS], [GH * T, PARTS * HD], [1, GH * T]])).then_inc(ready[b].sem, 16)
                        for r in range(PARTS):
                            sp.dma_start(KA[b][r * PARTS * HD:(r + 1) * PARTS * HD, :, :],
                                         at(k3_d, base + r * (LN_D * T), [[0, PARTS], [GH * T, HD], [1, GH * T]])).then_inc(ready[b].sem, 16)
                        flat = V_sb[:, b, :, :, :].rearrange("p g n c -> p g (n c)")
                        sp.dma_start(Vt[b][:, :, :].rearrange("p n c -> p (n c)"),
                                     flat[:, g, :] if isinstance(g, int) else flat[:, bass.ds(g, 1), :]).then_inc(ready[b].sem, 16)

                    if kind == "causal":
                        sp.dma_start(tab_m[:, 0, :], t["causal"]).then_inc(once.sem, 16)
                    for i in range(B):
                        sp.dma_start(KA[i][ROWS:ROWS + 1, :, :], t["ones"]).then_inc(once.sem, 16)
                    if full:
                        sp.dma_start(pick[:], t["pick"]).then_inc(once.sem, 16)

                    def load_tab_m(g):
                        for h in range(GH):
                            n = g * GH + h
                            sp.wait_ge(*tabm(n))
                            sp.dma_start(tab_f[:, 0, :], at(decay_t if full else biasr_t, n * (P * MW),
                                                            [[MW, P], [1, MW]])).then_inc(tabf.sem, 16)

                    def load_tab_e(g):
                        for h in range(GH):
                            if not isinstance(g, int) or g > 0:
                                sp.wait_ge(*biased(g * (B * U * GH)))
                            sp.dma_start(tab_e[:, h, :], at(decay_t if full else bias_t, (g * GH + h) * (P * MW),
                                                            [[MW, P], [1, MW]])).then_inc(tabe.sem, 16)

                    def store_row(b, it):
                        sp.wait_ge(*n_copied(it + 1))
                        sp.dma_start(QA[b][ROWS:ROWS + 1, :, :], nrow[:]).then_inc(n_stored.sem, 16)

                    load(0, 0)
                    if kind != "causal":
                        sp.wait_ge(*tables_made(16 * 3))
                        load_tab_m(0)
                        load_tab_e(0)
                    load(0, 1)
                    load(0, 2)
                    load(0, 3)
                    store_row(0, 0)

                    def body(g, b, last):
                        it = step_of(g, b)
                        more = not (isinstance(g, int) and g == G - 1)

                        def stores(I):
                            sp.wait_ge(*o_out(it * 2 + I + 1))
                            for h in range(GH):
                                sp.dma_start(at(ol_d, it * (GH * VW * T) + (h * VW * T + I * CH), [[T, VW], [1, CH]]),
                                             Ov[32 * h:32 * h + VW, I, :]).then_inc(o_stored[I].sem, 16)
                        stores(0)
                        if not last:
                            store_row((b + 1) % B, it + 1)
                        if more and b == B - 2 and kind != "causal":
                            load_tab_m(g + 1)
                        stores(1)
                        if more:
                            load(g + 1, b)
                            if b == B - 1 and kind != "causal":
                                load_tab_e(g + 1)
                    over_steps(sp, body)
                    for I in range(2):
                        sp.wait_ge(*o_stored[I](16 * GH * STEPS))

                @block.tensor
                def _(pe):
                    def first_scores(g, b, some):
                        it = step_of(g, b)
                        for n in some:
                            h, i, m, width = parts[n]
                            pe.wait_ge(*m_taken(it * NP + max(0, n - 2)))
                            nc.tensor.matmul(bank[M_BANKS[n % 3]][:, 0:width], QA[b][0:ROWS, h, i * P:(i + 1) * P],
                                             KA[b][0:ROWS, h, m * CH:m * CH + width], start=True,
                                             stop=True).then_inc(m_scores.sem, 1)

                    def turn_maxima(it):
                        pe.wait_ge(*n_ready(it + 1))
                        nc.tensor.transpose(bank[M_BANKS[0]][0:GH * TPB, 0:P], nmax[:], ident[:]).then_inc(n_turned.sem, 1)

                    def values(g, b, u):
                        it = step_of(g, b)
                        I, j, q0 = units[u]
                        pe.wait_ge(*exped((it * U + u + 1) * GH))
                        if u in diagonal:
                            pe.wait_ge(*masked(it * len(diagonal) + diagonal.index(u) + 1))
                        first = u == 0 or chunk_end[u - 1]
                        if first:
                            pe.wait_ge(*o_out(it * 2 + I))
                        for h in range(GH):
                            ins = nc.tensor.matmul(bank[O_BANK][32 * h:32 * h + VW, q0:CH],
                                                   Vt[b][:, j, h * VW:(h + 1) * VW], Ex[:, u % 2, h, 0:CH - q0],
                                                   start=first, stop=chunk_end[u])
                        ins.then_inc(summed.sem, 1)

                    def second_scores(g, b, u, h):
                        it = step_of(g, b)
                        I, j, q0 = units[u]
                        n = (it * U + u) * GH + h
                        pe.wait_ge(*exped(n - GH + 1 if b > 0 or u > 0 else n - h))
                        nc.tensor.matmul(bank[S_BANKS[h]][:, 0:CH - q0],
                                         KA[b][0:ROWS + (not full), h, j * P:(j + 1) * P],
                                         QA[b][0:ROWS + (not full), h, I * CH + q0:(I + 1) * CH],
                                         start=True, stop=True).then_inc(scores.sem, 1)

                    def lower_scores(g, b, u, h):
                        it = step_of(g, b)
                        I, j, q0 = units[u]
                        pe.wait_ge(*biased((it * U + u) * GH + h + 1))
                        nc.tensor.matmul(bank[S_BANKS[h]][:, :], pick[:], QA[b][0:ROWS + 1, h, I * CH:(I + 1) * CH],
                                         start=False, stop=True, skip_group_check=True).then_inc(lowered.sem, 1)

                    pe.wait_ge(*once(16 * NONCE))
                    pe.wait_ge(*ready[0](16 * NLOAD))
                    first_scores(0, 0, range(NP))
                    turn_maxima(0)

                    def body(g, b, last):
                        it = step_of(g, b)
                        nb = (b + 1) % B
                        ng = g + 1 if nb == 0 else g
                        pe.wait_ge(*n_stored(16 * (it + 1)))
                        pe.wait_ge(*filled(1))
                        if not last:
                            pe.wait_ge(*ready[nb]((ng + 1) * (16 * NLOAD)))
                        for u in range(U):
                            for h in range(GH):
                                second_scores(g, b, u, h)
                                if not last:
                                    first_scores(ng, nb, slot(u, h))
                                if full and h > 0:
                                    lower_scores(g, b, u, h - 1)
                            if full:
                                lower_scores(g, b, u, GH - 1)
                            if u > 0:
                                values(g, b, u - 1)
                            if not last and u == UM:
                                turn_maxima(it + 1)
                        values(g, b, U - 1)
                    over_steps(pe, body)

                @block.scalar
                def _(act):
                    def copy_row(it):
                        act.wait_ge(*n_turned(it + 1))
                        if not (isinstance(it, int) and it == 0):
                            act.wait_ge(*n_stored(16 * it))
                        nc.scalar.activation(nrow[:], bank[M_BANKS[0]][0:GH * TPB, 0:P], ACT.Copy).then_inc(n_copied.sem, 1)

                    copy_row(0)

                    def copy_output(it, I):
                        act.wait_ge(*summed(it * U + max(n for n, x in enumerate(units) if x[0] == I) + 1))
                        if not (isinstance(it, int) and it == 0):
                            act.wait_ge(*o_stored[I](it * (16 * GH)))
                        nc.scalar.activation(Ov[:, I, :], bank[O_BANK][:], ACT.Copy).then_inc(o_out.sem, 1)

                    def body(g, b, last):
                        it = step_of(g, b)
                        for u in range(U):
                            I, j, q0 = units[u]
                            for h in range(GH):
                                n = (it * U + u) * GH + h
                                act.wait_ge(*(scores if kind == "causal" else lowered if full else biased)(n + 1))
                                if h == 0 and b + u > 0:
                                    act.wait_ge(*summed(it * U + u - 1))
                                elif h == 0:
                                    act.wait_ge(*summed(it * U))
                                nc.scalar.activation(Ex[:, u % 2, h, 0:CH - q0], bank[S_BANKS[h]][:, 0:CH - q0],
                                                     ACT.Exp).then_inc(exped.sem, 1)
                            if u > 0 and chunk_end[u - 1]:
                                copy_output(it, 0)
                            if not last and u == UM:
                                copy_row(it + 1)
                        copy_output(it, 1)
                    over_steps(act, body)

                @block.vector
                def _(v):
                    nc.vector.memset(mx[:], NEG * 1e8)
                    nc.vector.memset(bank[O_BANK][:], 0.0).then_inc(filled.sem, 1)
                    v.wait_ge(*filled(1))
                    if kind == "causal":
                        v.wait_ge(*once(16 * NONCE))

                    def convert_tables(g):
                        for h in range(GH):
                            n = g * GH + h
                            v.wait_ge(*tabf(16 * (n + 1)))
                            nc.vector.tensor_copy(tab_m[:, h, :], tab_f[:, 0, :]).then_inc(tabm.sem, 1)
                        v.wait_ge(*tabm(g * GH + GH))

                    def maxima(it, some):
                        for n in some:
                            h, i, m, width = parts[n]
                            if not (isinstance(it, int) and it == 0 and n < 2):
                                v.wait_ge(*m_taken(it * NP + n - 1))
                            v.wait_ge(*m_scores(it * NP + n + 1))
                            v.sem_inc(m_seen.sem, 1)
                            c0 = CH * m + (TPB - 1 - i) * P
                            tab = tab_m[:, h if kind != "causal" else 0, c0:c0 + width]
                            nc.vector.tensor_tensor_reduce(out=waste[:, n % 2, 0:width], in0=bank[M_BANKS[n % 3]][:, 0:width],
                                                           in1=tab, scale=1.0, scalar=NEG * 1e8,
                                                           op0=ALU.mult if full else ALU.add, op1=ALU.max,
                                                           accum_out=mx[:, h * TPB + i, m:m + 1]).then_inc(m_taken.sem, 1)

                    def negate(it):
                        v.wait_ge(*m_taken((it + 1) * NP))
                        if not (isinstance(it, int) and it == 0):
                            v.wait_ge(*n_turned(it))
                        nc.vector.tensor_reduce(nmax[:], mx[:], AX.X, ALU.max, negate=True).then_inc(n_ready.sem, 1)

                    if kind != "causal":
                        convert_tables(0)
                    maxima(0, range(NP))
                    negate(0)

                    def body(g, b, last):
                        it = step_of(g, b)
                        nb = (b + 1) % B
                        if kind != "causal":
                            if b == 0:
                                v.wait_ge(*tabe((g + 1) * (16 * GH)))
                            if nb == 0 and not last:
                                convert_tables(g + 1)
                        for u in range(U):
                            I, j, q0 = units[u]
                            c0 = CH * I + q0 - P * j + (TABX - T if full else 0)
                            for h in range(GH):
                                if kind != "causal":
                                    v.wait_ge(*scores((it * U + u) * GH + h + 1))
                                    s = bank[S_BANKS[h]][:, 0:CH - q0]
                                    nc.vector.tensor_tensor(s, s, tab_e[:, h, c0:c0 + CH - q0],
                                                            ALU.mult if full else ALU.add).then_inc(biased.sem, 1)
                                if not last:
                                    maxima(it + 1, slot(u, h))
                            if not last and u == UM - 1:
                                negate(it + 1)
                    over_steps(v, body)

                if diagonal:
                    @block.gpsimd
                    def _(pool):
                        def body(g, b, last):
                            it = step_of(g, b)
                            for k, u in enumerate(diagonal):
                                pool.wait_ge(*exped((it * U + u + 1) * GH))
                                pool.sem_inc(d_seen.sem, 1)
                                tile = Ex[:, u % 2, :, 0:P]
                                nc.gpsimd.affine_select(out=tile, in_=tile, compare_op=ALU.is_ge, fill=0.0, base=0,
                                                        pattern=[[0, GH], [1, P]], channel_multiplier=-1).then_inc(masked.sem, 1)
                        over_steps(pool, body)

            D8 = len(diagonal)
            other = kind != "causal"
            for s in ready:
                s.close(16 * NLOAD * G)
            for s, n in ((once, 16 * NONCE), (filled, 1), (tabf, 16 * GH * G * other),
                         (tabm, GH * G * other), (tabe, 16 * GH * G * other), (m_scores, NP * STEPS), (m_taken, NP * STEPS),
                         (n_ready, STEPS), (n_turned, STEPS), (n_copied, STEPS), (n_stored, 16 * STEPS),
                         (scores, U * GH * STEPS), (biased, U * GH * STEPS * other), (lowered, U * GH * STEPS * full),
                         (exped, U * GH * STEPS), (masked, D8 * STEPS), (m_seen, NP * STEPS), (d_seen, D8 * STEPS), (summed, U * STEPS), (o_out, 2 * STEPS),
                         (o_stored[0], 16 * GH * STEPS), (o_stored[1], 16 * GH * STEPS)):
                s.close(n)

        def finish_attention(cfg):
            gated, biased = cfg["gated"], cfg["out_biased"]
            with ExitStack() as mem:
                den = sb("den", [P, CH], where=mem)
                inv = sb("inv", [P, CH], where=mem)
                w_o = sb("w_o", [P, P], where=mem)
                b_o = sb("b_o", [P, P], where=mem)
                O = sb("O", [P, 2, T], where=mem)
                R = sb("R", [P, 2, T], where=mem)
                N = sb("N", [P, 2, T], where=mem)
                loaded, den_in = sig("fa_loaded"), sig("fa_denominators")
                inverted, inv_stored = sig("fa_inverted"), sig("fa_inverses_stored")
                o_in = [sig("fa_output0"), sig("fa_output1")]
                gated_s, normed = sig("fa_gated"), sig("fa_normalised")
                made, added, bias_added = sig("fa_product"), sig("fa_added"), sig("fa_bias_added")
                block = mem.enter_context(nc.Block())
                NL = 1 + biased

                @block.sync
                def _(sp):
                    sp.dma_start(den[:], at(ol_d, HD * T, [[VW * T, G * B * GH], [CH, T // CH], [1, CH]])).then_inc(den_in.sem, 16)
                    sp.dma_start(w_o[:], cfg["w_o"]).then_inc(loaded.sem, 16)
                    if biased:
                        sp.dma_start(b_o[:], cfg["b_o"].partition_broadcast(P)).then_inc(loaded.sem, 16)
                    sp.wait_ge(*inverted(1))
                    sp.dma_start(rl_d.rearrange("r (m n) -> (r m) n", n=CH), inv[:]).then_inc(inv_stored.sem, 16)
                    sp.wait_ge(*inv_stored(16))
                    with sp.Fori(0, B // 2) as bb:
                        for s in range(2):
                            b = bb * 2 + s
                            sp.wait_ge(*normed(bb * 2))
                            for g in range(G):
                                rows = slice(g * GH * HD, (g + 1) * GH * HD)
                                sp.dma_start(O[rows, s, :], at(ol_d, b * (GH * VW * T) + g * B * GH * VW * T,
                                                               [[VW * T, GH], [T, HD], [1, T]])).then_inc(o_in[s].sem, 16)
                                sp.dma_start(R[rows, s, :], at(rl_d, b * (GH * T) + g * B * GH * T,
                                                               [[T, GH], [0, HD], [1, T]])).then_inc(o_in[s].sem, 16)

                @block.vector
                def _(v):
                    v.wait_ge(*den_in(16))
                    nc.vector.reciprocal(inv[:], den[:]).then_inc(inverted.sem, 1)
                    with v.Fori(0, B // 2) as bb:
                        for s in range(2):
                            b = bb * 2 + s
                            v.wait_ge(*o_in[s]((bb + 1) * (16 * 2 * G)))
                            v.wait_ge(*made(bb * 4))
                            if gated:
                                nc.vector.tensor_tensor(O[:, s, :], O[:, s, :], gate_sb[0][:, bass.ds(b * T, T)],
                                                        ALU.mult).then_inc(gated_s.sem, 1)
                                v.wait_ge(*gated_s(b + 1))
                            nc.vector.tensor_tensor(N[:, s, :], O[:, s, :], R[:, s, :], ALU.mult).then_inc(normed.sem, 1)
                            for c in range(2):
                                v.wait_ge(*made(b * 2 + c + 1))
                                if biased:
                                    v.wait_ge(*bias_added(NCH))
                                dst = x_sb[:, bass.ds(b * TPB + c * TPC, TPC), :]
                                nc.vector.tensor_tensor(dst, dst, bank[c][:, :].rearrange("p (n f) -> p n f", f=D),
                                                        ALU.add).then_inc(added.sem, 1)

                if biased:
                    @block.gpsimd
                    def _(pool):
                        pool.wait_ge(*loaded(16 * NL))
                        for c in range(NCH):
                            dst = x_sb[:, c * TPC:(c + 1) * TPC, :]
                            nc.gpsimd.tensor_tensor(dst, dst, b_o[:, :].unsqueeze(1).to_broadcast([P, TPC, D]),
                                                    ALU.add).then_inc(bias_added.sem, 1)

                @block.tensor
                def _(pe):
                    pe.wait_ge(*loaded(16 * NL))
                    with pe.Fori(0, B // 2) as bb:
                        for s in range(2):
                            b = bb * 2 + s
                            pe.wait_ge(*normed(b + 1))
                            for c in range(2):
                                pe.wait_ge(*added(b * 2))
                                for k in range(TPC):
                                    q = c * CH + k * P
                                    ins = nc.tensor.matmul(bank[c][:, k * P:(k + 1) * P], N[:, s, q:q + P], w_o[:],
                                                           start=True, stop=True)
                                ins.then_inc(made.sem, 1)

            for s, n in ((loaded, 16 * NL), (den_in, 16), (inverted, 1), (inv_stored, 16), (o_in[0], 16 * 4 * G),
                         (o_in[1], 16 * 4 * G), (gated_s, B * gated), (normed, B), (made, 2 * B), (added, 2 * B),
                         (bias_added, NCH * biased)):
                s.close(n)

        def route(cfg, mem_xT, weight):
            shared = cfg["shared"]
            NR = E + shared
            with ExitStack() as mem:
                w_r = sb("w_r", [P, NR], where=mem)
                logits = sb("logits", [P, TILES, NR], where=mem)
                top = sb("top", [P, 2, TILES], where=mem)
                place = sb("place", [P, 2, TILES], where=mem)
                second = sb("second", [P, TILES, E], where=mem)
                shifted = sb("shifted", [P, TILES, E], where=mem)
                hit = sb("hit", [P, 2, TILES, E], where=mem)
                number = sb("number", [P, E], where=mem)
                total = sb("total", [P, 2, TILES], where=mem)
                ln = norm_signals()
                loaded, made, kept = sig("ro_loaded"), sig("ro_logits"), sig("ro_logits_kept")
                xT_kept = sig("ro_transposed_kept")
                step, shift_ready, exp_ready = sig("ro_step"), sig("ro_shifted"), sig("ro_exp")
                block = mem.enter_context(nc.Block())

                @block.sync
                def _(sp):
                    sp.dma_start(w_r[:], cfg["w_r"]).then_inc(loaded.sem, 16)
                    sp.dma_start(number[:], t["number"].partition_broadcast(P)).then_inc(loaded.sem, 16)

                @block.tensor
                def _(pe):
                    pe.wait_ge(*loaded(32))
                    tensor_transpose(pe, ln, 0, 0)
                    with pe.Fori(0, NCH // 2) as cc:
                        for half in range(2):
                            c = cc * 2 + half
                            tensor_transpose(pe, ln, c + 1, 1 - half)
                            pe.wait_ge(*ln["copied"](c + 1))
                            pe.wait_ge(*kept(c))
                            for k in range(TPC):
                                ins = nc.tensor.matmul(bank[1][:, k * 16:k * 16 + NR], xTc[:, half, k * P:(k + 1) * P],
                                                       w_r[:], start=True, stop=True)
                            ins.then_inc(made.sem, 1)

                @block.scalar
                def _(act):
                    scalar_statistics(act, ln)

                    def copy_transposed(c, slot):
                        act.wait_ge(*ln["transposed"](c + 1))
                        if not isinstance(c, int):
                            act.wait_ge(*made(c - 1))
                            act.wait_ge(*xT_kept(c - 1))
                        nc.scalar.activation(xTc[:, slot, :], bank[0][:], ACT.Copy).then_inc(ln["copied"].sem, 1)
                    copy_transposed(0, 0)
                    with act.Fori(0, NCH // 2) as cc:
                        for half in range(2):
                            c = cc * 2 + half
                            copy_transposed(c + 1, 1 - half)
                            act.wait_ge(*ln["copied"](c + 1))
                            nc.scalar.activation(mem_xT[:, bass.ds(c * CH, CH)], xTc[:, half, :], ACT.Copy).then_inc(xT_kept.sem, 1)
                    act.wait_ge(*shift_ready(1))
                    nc.scalar.activation(shifted[:], shifted[:], ACT.Exp).then_inc(exp_ready.sem, 1)
                    if shared:
                        nc.scalar.activation(total[:, 1, :], logits[:, :, E], ACT.Exp, scale=-1.0).then_inc(exp_ready.sem, 1)

                @block.vector
                def _(v):
                    vector_statistics(v, ln)
                    vector_normalise(v, ln, 0, 0)
                    with v.Fori(0, NCH // 2) as cc:
                        for half in range(2):
                            c = cc * 2 + half
                            vector_normalise(v, ln, c + 1, 1 - half)
                            v.wait_ge(*made(c + 1))
                            nc.vector.tensor_copy(logits[:, bass.ds(c * TPC, TPC), :],
                                                  bank[1][:, 0:TPC * 16].rearrange("p (n f) -> p n f", f=16)[:, :, 0:NR]).then_inc(kept.sem, 1)
                    v.wait_ge(*kept(NCH))
                    v.wait_ge(*loaded(32))
                    done = [0]

                    def chained(ins):
                        done[0] += 1
                        ins.then_inc(step.sem, 1)
                        v.wait_ge(*step(done[0]))

                    wide = [P, TILES, E]
                    countdown = number[:, :].unsqueeze(1).to_broadcast(wide)
                    for n in range(2):
                        src = logits[:, :, 0:E] if n == 0 else second[:]
                        chained(nc.vector.tensor_reduce(top[:, n, :], src, AX.X, ALU.max))
                        if n == 0:
                            nc.vector.tensor_tensor(shifted[:], src, top[:, 0, :].unsqueeze(2).to_broadcast(wide),
                                                    ALU.subtract).then_inc(shift_ready.sem, 1)
                        chained(nc.vector.tensor_tensor(hit[:, n, :, :], src, top[:, n, :].unsqueeze(2).to_broadcast(wide),
                                                        ALU.is_equal))
                        chained(nc.vector.tensor_tensor(hit[:, n, :, :], hit[:, n, :, :], countdown, ALU.mult))
                        chained(nc.vector.tensor_reduce(place[:, n, :], hit[:, n, :, :], AX.X, ALU.max))
                        chained(nc.vector.tensor_tensor(hit[:, n, :, :], countdown,
                                                        place[:, n, :].unsqueeze(2).to_broadcast(wide), ALU.is_equal))
                        if n == 0:
                            chained(nc.vector.tensor_scalar(second[:], hit[:, 0, :, :], NEG, None, ALU.mult))
                            chained(nc.vector.tensor_tensor(second[:], second[:], logits[:, :, 0:E], ALU.add))
                    chained(nc.vector.tensor_tensor(hit[:, 0, :, :], hit[:, 0, :, :], hit[:, 1, :, :], ALU.add))
                    v.wait_ge(*exp_ready(1 + shared))
                    if shared:
                        chained(nc.vector.tensor_scalar(total[:, 1, :], total[:, 1, :], 1.0, None, ALU.add))
                        chained(nc.vector.reciprocal(weight[:, :, E], total[:, 1, :]))
                    chained(nc.vector.reduce_sum(total[:, 0, :], shifted[:], AX.X))
                    chained(nc.vector.reciprocal(total[:, 0, :], total[:, 0, :]))
                    chained(nc.vector.tensor_tensor(hit[:, 0, :, :], hit[:, 0, :, :], shifted[:], ALU.mult))
                    chained(nc.vector.tensor_tensor(weight[:, :, 0:E], hit[:, 0, :, :],
                                                    total[:, 0, :].unsqueeze(2).to_broadcast(wide), ALU.mult))
                    steps[0] = done[0]
            close_norm(ln)
            for s, n in ((loaded, 32), (made, NCH), (kept, NCH), (xT_kept, NCH), (step, steps[0]), (shift_ready, 1),
                         (exp_ready, 1 + shared)):
                s.close(n)

        steps = [0]

        def experts(cfg, xT, weight):
            shared = cfg["shared"]
            NR = E + shared
            NE = E + shared
            act_fn = ACT.Silu if shared else ACT.Gelu_apprx_tanh
            with ExitStack() as mem:
                w_up = sb("w_up", [P, E + 2 * shared, P], where=mem)
                w_down = sb("w_down", [P, NE, P], where=mem)
                b_up = sb("b_up", [P, E], where=mem)
                b_down = sb("b_down", [P, CH], where=mem)
                h = sb("h", [P, 2, CH], where=mem)
                gate = sb("gate", [P, CH], where=mem) if shared else None
                wst = sb("wst", [P, 2, P], where=mem)
                wT = sb("wT", [P, 2, P], where=mem)
                loaded, filled = sig("ex_loaded"), sig("ex_filled")
                up, active, down, added = sig("ex_up"), sig("ex_active"), sig("ex_down"), sig("ex_added")
                gated, up_shared, gate_done = sig("ex_gated"), sig("ex_up_shared"), sig("ex_gate")
                staged, turned, wT_ready, bias_made = sig("ex_weights_staged"), sig("ex_weights_turned"), sig("ex_weights_ready"), sig("ex_bias")
                block = mem.enter_context(nc.Block())
                NL = 2 if shared else 3 + TPC
                ADDS = NE * TPC + (not shared)
                H_BANKS, GATE_BANK, UP_BANK, Y_BANKS, B_BANK = (0, 1), 2, 3, (4, 5), 6

                @block.sync
                def _(sp):
                    sp.dma_start(w_up[:], cfg["w_up"].rearrange("p (e f) -> p e f", f=P)).then_inc(loaded.sem, 16)
                    sp.dma_start(w_down[:], cfg["w_down"].rearrange("p (e f) -> p e f", f=P)).then_inc(loaded.sem, 16)
                    if not shared:
                        sp.dma_start(b_up[:], cfg["b_up"]).then_inc(loaded.sem, 16)
                        sp.wait_ge(*filled(1))
                        for k in range(TPC):
                            sp.dma_start(b_down[k * E:(k + 1) * E, k * P:(k + 1) * P], cfg["b_down"]).then_inc(loaded.sem, 16)

                if not shared:
                    @block.gpsimd
                    def _(pool):
                        nc.gpsimd.memset(b_down[:], 0.0).then_inc(filled.sem, 1)
                        nc.gpsimd.memset(wst[:], 0.0).then_inc(filled.sem, 1)
                        pool.wait_ge(*filled(2))
                        with pool.Fori(0, NCH // 2) as cc:
                            for half in range(2):
                                c = cc * 2 + half
                                pool.wait_ge(*turned(cc * 2))
                                nc.gpsimd.tensor_copy(wst[:, half, 0:TPC * E].rearrange("p (n e) -> p n e", e=E),
                                                      weight[:, bass.ds(c * TPC, TPC), 0:E]).then_inc(staged.sem, 1)

                @block.tensor
                def _(pe):
                    pe.wait_ge(*loaded(16 * NL))

                    def down_products(c, half, e):
                        d = half * NE + e
                        pe.wait_ge(*(active(c * E + e + 1) if e < E else gated(c + 1)))
                        pe.wait_ge(*added_before(c, half, e))
                        for k in range(TPC):
                            ins = nc.tensor.matmul(bank[Y_BANKS[d % 2]][:, k * P:(k + 1) * P],
                                                   h[:, d % 2, k * P:(k + 1) * P], w_down[:, e, :], start=True, stop=True)
                        ins.then_inc(down.sem, 1)

                    def added_before(c, half, e):
                        if e >= 2:
                            return added(c * ADDS + (e - 1) * TPC)
                        return added(c * ADDS if half == 0 else c * ADDS - (not shared) - (1 - e) * TPC)

                    with pe.Fori(0, NCH // 2) as cc:
                        for half in range(2):
                            c = cc * 2 + half
                            moving = xT[:, bass.ds(c * CH, CH)]
                            for e in range(NE):
                                if e < E:
                                    pe.wait_ge(*active(c * E + (e - 1 if e >= 2 else 0)))
                                    nc.tensor.matmul(bank[H_BANKS[e % 2]][:], w_up[:, e, :], moving, start=True,
                                                     stop=True).then_inc(up.sem, 1)
                                else:
                                    pe.wait_ge(*gated(c))
                                    for i, bk in ((E, GATE_BANK), (E + 1, UP_BANK)):
                                        ins = nc.tensor.matmul(bank[bk][:], w_up[:, i, :], moving, start=True, stop=True)
                                    ins.then_inc(up_shared.sem, 1)
                                if e > 0:
                                    down_products(c, half, e - 1)
                                if e == 3 and not shared:
                                    pe.wait_ge(*staged(c + 1))
                                    pe.wait_ge(*added(c * ADDS))
                                    nc.tensor.transpose(bank[B_BANK][:, 0:P], wst[:, half, :], ident[:]).then_inc(turned.sem, 1)
                                if e == 6 and not shared:
                                    pe.wait_ge(*wT_ready(c + 1))
                                    nc.tensor.matmul(bank[B_BANK][:], wT[:, half, :], b_down[:], start=True,
                                                     stop=True).then_inc(bias_made.sem, 1)
                            down_products(c, half, NE - 1)

                @block.scalar
                def _(act):
                    act.wait_ge(*loaded(16 * NL))
                    with act.Fori(0, NCH // 2) as cc:
                        for half in range(2):
                            c = cc * 2 + half
                            for e in range(E):
                                n, d = c * NE + e, half * NE + e
                                act.wait_ge(*up(c * E + e + 1))
                                act.wait_ge(*down(n - 1 if e >= 2 or half else c * NE))
                                if shared:
                                    ins = nc.scalar.activation(h[:, d % 2, :], bank[H_BANKS[e % 2]][:], act_fn)
                                else:
                                    ins = nc.scalar.activation(h[:, d % 2, :], bank[H_BANKS[e % 2]][:], act_fn,
                                                               bias=b_up[:, e:e + 1])
                                ins.then_inc(active.sem, 1)
                                if e == 4 and not shared:
                                    act.wait_ge(*turned(c + 1))
                                    act.wait_ge(*bias_made(c))
                                    nc.scalar.activation(wT[:, half, :], bank[B_BANK][:, 0:P], ACT.Copy).then_inc(wT_ready.sem, 1)
                            if shared:
                                act.wait_ge(*up_shared(c + 1))
                                act.wait_ge(*gated(c))
                                nc.scalar.activation(gate[:], bank[GATE_BANK][:], act_fn).then_inc(gate_done.sem, 1)

                @block.vector
                def _(v):
                    with v.Fori(0, NCH // 2) as cc:
                        for half in range(2):
                            c = cc * 2 + half
                            x_c = [x_sb[:, bass.ds(c * TPC + k, 1), :] for k in range(TPC)]
                            for e in range(NE):
                                d = half * NE + e
                                if e == E:
                                    v.wait_ge(*gate_done(c + 1))
                                    v.wait_ge(*down(c * NE + E - 1))
                                    nc.vector.tensor_tensor(h[:, d % 2, :], gate[:], bank[UP_BANK][:],
                                                            ALU.mult).then_inc(gated.sem, 1)
                                v.wait_ge(*down(c * NE + e + 1))
                                for k in range(TPC):
                                    if e > 0:
                                        v.wait_ge(*added(c * ADDS + (e - 1) * TPC + k + 1))
                                    nc.vector.scalar_tensor_tensor(out=x_c[k], in0=bank[Y_BANKS[d % 2]][:, k * P:(k + 1) * P].unsqueeze(1),
                                                                   scalar=weight[:, bass.ds(c * TPC + k, 1), e], in1=x_c[k],
                                                                   op0=ALU.mult, op1=ALU.add).then_inc(added.sem, 1)
                            if not shared:
                                v.wait_ge(*added(c * ADDS + NE * TPC))
                                v.wait_ge(*bias_made(c + 1))
                                dst = x_sb[:, bass.ds(c * TPC, TPC), :]
                                nc.vector.tensor_tensor(dst, dst, bank[B_BANK][:, :].rearrange("p (n f) -> p n f", f=D),
                                                        ALU.add).then_inc(added.sem, 1)
            for s, n in ((loaded, 16 * NL), (filled, 2 * (not shared)), (up, NCH * E), (active, NCH * E), (gated, NCH * shared), (down, NCH * NE),
                         (added, NCH * ADDS), (up_shared, NCH * shared), (gate_done, NCH * shared),
                         (staged, NCH * (not shared)), (turned, NCH * (not shared)), (wT_ready, NCH * (not shared)),
                         (bias_made, NCH * (not shared))):
                s.close(n)

        def epilogue():
            with ExitStack() as mem:
                stored = sig("x_stored")
                block = mem.enter_context(nc.Block())

                @block.sync
                def _(sp):
                    sp.dma_start(out.rearrange("(n p) f -> p n f", p=P), x_sb[:, 0:TILES, :]).then_inc(stored.sem, 16)
                    sp.wait_ge(*stored(16))

        gate_sb = [None]

        def attention(cfg):
            with ExitStack() as mem:
                if cfg["gated"]:
                    gate_sb[0] = sb("gate_sb", [P, B * T], where=mem)
                project(cfg)
                attend(cfg)
                finish_attention(cfg)

        def moe(cfg):
            with ExitStack() as mem:
                xT = sb("xT", [P, B * T], where=mem)
                weight = sb("weight", [P, TILES, E + 1], where=mem)
                route(cfg, xT, weight)
                experts(cfg, xT, weight)

        attentions = [
            dict(kind="causal", rope=False, biased=False, gated=False, out_biased=True, w=t["w0"], nw=3,
                 w_o=t["wo0"], b_o=t["bo0"]),
            dict(kind="decay", rope=False, biased=True, gated=False, out_biased=True, w=t["w1"], nw=3,
                 b_qk=t["bqk1"], b_v=t["bv1"], w_o=t["wo1"], b_o=t["bo1"]),
            dict(kind="sparse", rope=False, biased=True, gated=True, out_biased=True, w=t["w2"], nw=4,
                 b_qk=t["bqk2"], b_v=t["bv2"], w_o=t["wo2"], b_o=t["bo2"]),
            dict(kind="causal", rope=True, biased=False, gated=False, out_biased=False, w=t["w3"], nw=5,
                 w_o=t["wo3"]),
        ]
        ffn0 = dict(shared=0, w_r=t["wr0"], w_up=t["wup0"], w_down=t["wdn0"], b_up=t["bup0"], b_down=t["bdn0"])
        ffn1 = dict(shared=1, w_r=t["wr1"], w_up=t["wup1"], w_down=t["wdn1"])

        prologue()
        for n, ffn in enumerate((ffn0, ffn0, ffn1, ffn1)):
            attention(attentions[n])
            moe(ffn)
        epilogue()


def kernel(**inputs):
    import numpy as np
    import concourse.bacc as bacc
    from concourse.bass_utils import run_bass_kernel_spmd

    def get(name):
        return np.asarray(inputs[name])

    perm = np.array([(GH * g + h) * HD + d for g in range(G) for d in range(HD) for h in range(GH)])
    swap = np.array([(GH * g + h) * HD + (d ^ 1) for g in range(G) for d in range(HD) for h in range(GH)])

    def side_by_side(*parts):
        return np.ascontiguousarray(np.concatenate(parts, axis=1))

    def column(*rows):
        return np.ascontiguousarray(np.stack(rows, axis=1))

    def experts(w):
        return np.ascontiguousarray(w.transpose(1, 0, 2).reshape(P, -1))

    f32, half_type = np.float32, mybir.dt.np(bf16)
    a = {}
    a["x"] = np.ascontiguousarray(get("L0_attn_a_x").reshape(B * T, D))
    a["ident"] = np.eye(P, dtype=f32)
    cols = np.arange(T) - (T - P)
    a["causal"] = np.where(cols[None, :] > np.arange(P)[:, None], f32(NEG), f32(0)).astype(half_type)
    a["ones"] = np.ones((1, GH * T), dtype=half_type)
    pick = np.zeros((ROWS + 1, P), dtype=f32)
    pick[ROWS] = 1
    a["pick"] = pick.astype(half_type)
    a["dist"] = np.abs(np.arange(ROWX) - (T - 1)).astype(f32)[None, :]
    a["delta"] = (np.arange(T + 127) - 127).astype(f32)[None, :]
    a["deltar"] = (T - 1 - np.arange(T + 127)).astype(f32)[None, :]
    a["number"] = (E - np.arange(E)).astype(f32)[None, :]
    inv_freq = (f32(1) / (f32(10000) ** (np.arange(0, HD, 2).astype(f32) / f32(HD)))).astype(f32)
    angle = (np.arange(T).astype(f32)[:, None] * inv_freq[None, :]).astype(f32).astype(np.float64)
    dims = np.array([d for g in range(G) for d in range(HD) for h in range(GH)])
    cos = np.cos(angle)[:, dims // 2].T
    sin = (np.sin(angle)[:, dims // 2] * np.where(dims % 2, 1.0, -1.0)[None, :]).T
    a["turn"] = np.ascontiguousarray(np.concatenate([cos * SCALE, cos, sin * SCALE, sin], axis=1).astype(f32))
    wq, wk, wv = np.split(get("L0_attn_a_w_qkv"), 3, axis=1)
    a["w0"] = side_by_side(wq[:, perm], wk[:, perm], wv)
    a["wo0"], a["bo0"] = get("L0_attn_a_w_out"), get("L0_attn_a_b_out")[None, :]
    a["w1"] = side_by_side(get("L0_attn_b_Wq").T[:, perm], get("L0_attn_b_Wk").T[:, perm], get("L0_attn_b_Wv").T)
    bq, bk = get("L0_attn_b_bq"), get("L0_attn_b_bk")
    a["bqk1"] = column(bq[perm], bk[perm], bk)
    a["bv1"] = get("L0_attn_b_bv")[None, :]
    a["wo1"], a["bo1"] = np.ascontiguousarray(get("L0_attn_b_Wo").T), get("L0_attn_b_bo")[None, :]
    a["decay"], a["mix"] = get("L0_attn_b_decay_params"), get("L0_attn_b_mix_weights")
    wq, wk, wv = np.split(get("L1_attn_a_Wqkv").T, 3, axis=1)
    bq, bk, bv = np.split(get("L1_attn_a_bqkv"), 3)
    a["w2"] = side_by_side(wq[:, perm], wk[:, perm], wv, get("L1_attn_a_Wgate").T)
    a["bqk2"] = column(bq[perm], bk[perm], get("L1_attn_a_bgate"))
    a["bv2"] = bv[None, :]
    a["wo2"], a["bo2"] = np.ascontiguousarray(get("L1_attn_a_Wout").T), get("L1_attn_a_bout")[None, :]
    a["pos_bias"] = get("L1_attn_a_pos_bias")
    a["pos_biasT"] = np.ascontiguousarray(a["pos_bias"].T)
    a["offsets"] = get("L1_attn_a_offsets")[:, None]
    q, k = get("L1_attn_b_qw"), get("L1_attn_b_kw")
    a["w3"] = side_by_side(q[:, perm], k[:, perm], q[:, swap], k[:, swap], get("L1_attn_b_vw"))
    a["wo3"] = get("L1_attn_b_ow")
    a["wr0"] = get("L0_ffn_router_w")
    a["wup0"], a["wdn0"] = experts(get("L0_ffn_w_in")), experts(get("L0_ffn_w_out"))
    a["bup0"], a["bdn0"] = np.ascontiguousarray(get("L0_ffn_b_in").T), get("L0_ffn_b_out")
    a["wr1"] = side_by_side(get("L1_ffn_router_w"), get("L1_ffn_shared_gate_w"))
    a["wup1"] = side_by_side(experts(get("L1_ffn_w1")), get("L1_ffn_shared_gate_up"))
    a["wdn1"] = side_by_side(experts(get("L1_ffn_w2")), get("L1_ffn_shared_down"))

    nc = bacc.Bacc("TRN2", target_bir_lowering=False, num_devices=1)
    arrays, tensors = {}, {}
    for name, value in a.items():
        value = np.ascontiguousarray(value)
        arrays[f"in_{name}"] = value
        tensors[name] = nc.dram_tensor(f"in_{name}", value.shape, mybir.dt.from_np(value.dtype), kind="ExternalInput").ap()
    out = nc.dram_tensor("out_x", (B * T, D), fp32, kind="ExternalOutput").ap()
    hybrid_program(nc, tensors, out)
    r = run_bass_kernel_spmd(nc, [arrays], core_ids=[0])
    return r.results[0]["out_x"].reshape(B, T, D)
```

```python
import concourse.bass as bass
from concourse import mybir
from contextlib import ExitStack

fp32 = mybir.dt.float32
bf16 = mybir.dt.bfloat16
i32 = mybir.dt.int32
ALU = mybir.AluOpType
ACT = mybir.ActivationFunctionType
AX = mybir.AxisListType

B, T, D = 4, 1024, 128
H, HD = 16, 8
E = 8
P = 128
TILES = B * T // P
TPB = T // P
CH = 512
TPC = CH // P
NCH = B * T // CH
G, GH = 4, 4
PARTS = 3
ROWS = PARTS * PARTS * HD
VW = HD + 1
NEG = -1.0e30
SCALE = float(HD) ** -0.5
EPS = 1e-5
LN_D = 32
NOFF = 68
TABX = 1920
NEAR0 = TABX - T - (CH - P)
ROWX = TABX + 127
FAR_TERMS = 6
FAR_ROWS = FAR_TERMS * 2 * HD


class Signal:

    def __init__(self, sem):
        self.sem, self.base = sem, 1

    def __call__(self, n):
        return self.sem, self.base + n

    def close(self, total):
        self.base += total


def hybrid_program(nc, t, out):
    ctx = ExitStack()
    with ctx:
        used = {}

        def sb(name, shape, dt=fp32, where=ctx):
            used[name] = used.get(name, 0) + 1
            name += f"_{used[name]}" if used[name] > 1 else ""
            return where.enter_context(nc.sbuf_tensor(name, shape, dt))

        def dram(name, shape, dt=fp32):
            return nc.dram_tensor(name, shape, dt, kind="Internal").ap()

        signals = {}

        def sig(name):
            if name not in signals:
                signals[name] = Signal(ctx.enter_context(nc.semaphore(name)))
                nc.sync.sem_inc(signals[name].sem, 1)
            return signals[name]

        x_sb = sb("x_sb", [P, TILES + TPC, D])
        stats = sb("stats", [P, TILES, 6])
        meanvar = sb("meanvar", [P, TILES + TPC, 2])
        rstd = sb("rstd", [P, TILES + TPC])
        ident = sb("ident", [P, P])
        eps = sb("eps", [P, 1])
        V_sb = sb("V_sb", [P, B, G, TPB, GH * VW])
        bank = [ctx.enter_context(nc.psum_tensor(f"bank{i}", [P, CH], fp32)) for i in range(8)]

        q3_d = dram("q3_d", [G * B, PARTS, LN_D * T], bf16)
        k3_d = dram("k3_d", [G * B, PARTS, LN_D * T], bf16)
        q6_d = dram("q6_d", [G * B, PARTS, 2 * LN_D * T], bf16)
        k6_d = dram("k6_d", [G * B, PARTS, 2 * LN_D * T], bf16)
        far_d = dram("far_d", [H, 4 * T])
        ol_d = dram("ol_d", [B, H, VW, T])
        rl_d = dram("rl_d", [B * H, T])
        decay_d = dram("decay_d", [H, ROWX])
        bias_d = dram("bias_d", [H, T + 127])
        decayb_d = dram("decayb_d", [H, ROWX], bf16)
        biasr_d = dram("biasr_d", [H, T + 127], bf16)
        decay_t = dram("decay_t", [H, P, T])
        bias_t = dram("bias_t", [H, P, T])
        decayb_t = dram("decayb_t", [H, P, TABX], bf16)
        biasr_t = dram("biasr_t", [H, P, T], bf16)
        biasp_d = dram("biasp_d", [H, PARTS * (T + 127)], bf16)
        biasp_t = dram("biasp_t", [G, PARTS, P, T], bf16)
        tables_made = sig("tables_made")

        def at(ap, offset, dims):
            return bass.AP(ap.tensor, offset, dims)

        def prologue():
            W = T + 127
            with ExitStack() as mem:
                mixes = sb("mixes", [H, 2], where=mem)
                clip = sb("clip", [H, 2], where=mem)
                lndp = sb("lndp", [H, 2], where=mem)
                mix_nmax = sb("mix_nmax", [H, 1], where=mem)
                mix_exp = sb("mix_exp", [H, 2], where=mem)
                mix_sum = sb("mix_sum", [H, 2], where=mem)
                mix = sb("mix", [H, 2], where=mem)
                dist = sb("dist", [H, ROWX], where=mem)
                power = sb("power", [H, 2, ROWX], where=mem)
                decay_row = sb("decay_row", [H, ROWX], where=mem)
                decay_row_b = sb("decay_row_b", [H, ROWX], bf16, where=mem)
                row_b = sb("row_b", [H, W], bf16, where=mem)
                row_parts = sb("row_parts", [H, PARTS, W], bf16, where=mem)
                row_rest = sb("row_rest", [H, W], where=mem)
                far_q = sb("far_q", [H, 2, T], where=mem)
                off_i = sb("off_i", [NOFF, 1], i32, where=mem)
                off_f = sb("off_f", [NOFF, 1], where=mem)
                pbT = sb("pbT", [H, NOFF], where=mem)
                pb_nmax = sb("pb_nmax", [H, 1], where=mem)
                pexp = sb("pexp", [H, NOFF], where=mem)
                three = sb("three", [NOFF, 96], where=mem)
                deltas = sb("deltas", [NOFF, 2, W], where=mem)
                hot = sb("hot", [NOFF, 2, W], where=mem)
                count = sb("count", [H, 2, W], where=mem)
                single = sb("single", [H, 2, W], where=mem)
                esum = sb("esum", [H, 2, W], where=mem)
                lse = sb("lse", [H, 2, W], where=mem)
                flag = sb("flag", [H, 2, W], where=mem)
                row = sb("row", [H, 2, W], where=mem)
                loaded, filled, three_set = sig("pro_loaded"), sig("pro_filled"), sig("pro_three_set")
                vstep = sig("pro_vstep")
                logs, mixexp, powers, pbexp, lse_done = (sig("pro_logs"), sig("pro_mixexp"), sig("pro_powers"),
                                                         sig("pro_pbexp"), sig("pro_lse"))
                pexpT, sums, stored = sig("pro_pexpT"), sig("pro_sums"), sig("pro_stored")
                clipped, mixed, decays_ready, biasmax, hot_ready, esum_ready, rows_ready = (
                    sig(n) for n in ("pro_clipped", "pro_mixed", "pro_decays", "pro_biasmax", "pro_hot",
                                     "pro_esum", "pro_rows"))
                block = mem.enter_context(nc.Block())
                LOADS = 10
                cuts = [(a, min(a + CH, W)) for a in range(0, W, CH)]

                @block.sync
                def _(sp):
                    for dst, src in ((x_sb[:, 0:TILES, :], t["x"].rearrange("(n p) f -> p n f", p=P)),
                                     (ident[:], t["ident"]), (clip[:], t["decay"]), (mixes[:], t["mix"]),
                                     (dist[:], t["dist"].partition_broadcast(H)), (off_i[:], t["offsets"]),
                                     (pbT[:], t["pos_biasT"]), (three[:, 32:32 + H], t["pos_bias"]),
                                     (deltas[:, 0, :], t["delta"].partition_broadcast(NOFF)),
                                     (deltas[:, 1, :], t["deltar"].partition_broadcast(NOFF))):
                        if dst.tensor.name == three.name:
                            sp.wait_ge(*three_set(1))
                        sp.dma_start(dst, src).then_inc(loaded.sem, 16)
                    sp.wait_ge(*decays_ready(4))
                    sp.dma_start(decay_d, decay_row[:]).then_inc(stored.sem, 16)
                    sp.dma_start(far_d[:, 0:2 * T], far_q[:, :, :].rearrange("p n t -> p (n t)")).then_inc(stored.sem, 16)
                    sp.dma_start(far_d[:, 2 * T:4 * T].rearrange("p (n t) -> p n t", t=T),
                                 power[:, :, T - 1 - CH:2 * T - 1 - CH]).then_inc(stored.sem, 16)
                    sp.dma_start(decayb_d, decay_row_b[:]).then_inc(stored.sem, 16)
                    sp.wait_ge(*rows_ready(3))
                    sp.dma_start(bias_d, row[:, 0, :]).then_inc(stored.sem, 16)
                    sp.dma_start(biasr_d, row_b[:]).then_inc(stored.sem, 16)
                    sp.dma_start(biasp_d, row_parts[:, :, :].rearrange("p a w -> p (a w)")).then_inc(stored.sem, 16)
                    sp.wait_ge(*stored(16 * 7))

                @block.gpsimd
                def _(pool):
                    nc.gpsimd.memset(three[:], 1.0).then_inc(three_set.sem, 1)
                    nc.gpsimd.memset(V_sb[:], 1.0).then_inc(filled.sem, 1)
                    nc.gpsimd.memset(x_sb[:, TILES:TILES + TPC, :], 0.0).then_inc(filled.sem, 1)
                    nc.gpsimd.memset(meanvar[:, TILES:TILES + TPC, :], 0.0).then_inc(filled.sem, 1)
                    nc.gpsimd.memset(rstd[:, TILES:TILES + TPC], 1.0).then_inc(filled.sem, 1)
                    nc.gpsimd.memset(eps[:], EPS).then_inc(filled.sem, 1)

                @block.vector
                def _(v):
                    done = [0]

                    def step(ins):
                        done[0] += 1
                        ins.then_inc(vstep.sem, 1)
                        v.wait_ge(*vstep(done[0]))

                    v.wait_ge(*loaded(16 * LOADS))
                    step(nc.vector.tensor_scalar(clip[:], clip[:], 0.01, 0.9999, ALU.max, ALU.min))
                    nc.vector.tensor_reduce(mix_nmax[:], mixes[:], AX.X, ALU.max, negate=True).then_inc(clipped.sem, 1)
                    nc.vector.tensor_reduce(pb_nmax[:], pbT[:], AX.X, ALU.max, negate=True).then_inc(biasmax.sem, 1)
                    step(nc.vector.tensor_copy(off_f[:], off_i[:]))
                    nc.vector.tensor_scalar(hot[:, :, :], deltas[:, :, :], off_f[:, 0:1], None,
                                            ALU.is_equal).then_inc(hot_ready.sem, 1)
                    v.wait_ge(*pexpT(1))
                    nc.vector.tensor_copy(three[:, 64:64 + H], bank[7][0:NOFF, 0:H]).then_inc(hot_ready.sem, 1)
                    v.wait_ge(*mixexp(1))
                    step(nc.vector.reduce_sum(mix_sum[:, 0:1], mix_exp[:], AX.X))
                    step(nc.vector.reciprocal(mix_sum[:, 1:2], mix_sum[:, 0:1]))
                    step(nc.vector.tensor_scalar(mix[:], mix_exp[:], mix_sum[:, 1:2], None, ALU.mult))
                    v.wait_ge(*powers(2))
                    for n in range(2):
                        nc.vector.tensor_scalar(far_q[:, n, :], power[:, n, T - 1 - CH:2 * T - 1 - CH], mix[:, n:n + 1],
                                                None, ALU.mult).then_inc(decays_ready.sem, 1)
                    step(nc.vector.tensor_scalar(decay_row[:], power[:, 1, :], mix[:, 1:2], None, ALU.mult))
                    nc.vector.scalar_tensor_tensor(out=decay_row[:], in0=power[:, 0, :], scalar=mix[:, 0:1],
                                                   in1=decay_row[:], op0=ALU.mult,
                                                   op1=ALU.add).then_inc(decays_ready.sem, 1)
                    v.wait_ge(*decays_ready(3))
                    nc.vector.tensor_copy(decay_row_b[:], decay_row[:]).then_inc(decays_ready.sem, 1)
                    for r in range(2):
                        for c, (a, b) in enumerate(cuts):
                            k = r * len(cuts) + c
                            v.wait_ge(*sums(k + 1))
                            nc.vector.tensor_copy(count[:, r, a:b], bank[k][0:H, 0:b - a])
                            nc.vector.tensor_copy(single[:, r, a:b], bank[k][32:32 + H, 0:b - a])
                            step(nc.vector.tensor_scalar(esum[:, r, a:b], bank[k][64:64 + H, 0:b - a],
                                                         1e-18, None, ALU.max))
                    nc.vector.tensor_scalar(flag[:], count[:], 1.5, None, ALU.is_gt).then_inc(esum_ready.sem, 1)
                    v.wait_ge(*lse_done(1))
                    step(nc.vector.tensor_scalar(lse[:], lse[:], pb_nmax[:, 0:1], None, ALU.subtract))
                    step(nc.vector.tensor_tensor(lse[:], lse[:], single[:], ALU.subtract))
                    step(nc.vector.tensor_tensor(lse[:], lse[:], flag[:], ALU.mult))
                    step(nc.vector.tensor_tensor(lse[:], lse[:], single[:], ALU.add))
                    step(nc.vector.tensor_scalar(flag[:], count[:], 0.5, NEG, ALU.is_lt, ALU.mult))
                    nc.vector.tensor_tensor(row[:], lse[:], flag[:], ALU.add).then_inc(rows_ready.sem, 1)
                    v.wait_ge(*rows_ready(1))
                    nc.vector.tensor_copy(row_b[:], row[:, 1, :]).then_inc(rows_ready.sem, 1)
                    step(nc.vector.tensor_copy(row_parts[:, 0, :], row[:, 0, :]))
                    step(nc.vector.tensor_tensor(row_rest[:], row[:, 0, :], row_parts[:, 0, :], ALU.subtract))
                    step(nc.vector.tensor_copy(row_parts[:, 1, :], row_rest[:]))
                    nc.vector.tensor_tensor(row_parts[:, 2, :], row_rest[:], row_parts[:, 1, :], ALU.subtract).then_inc(rows_ready.sem, 1)

                @block.scalar
                def _(act):
                    act.wait_ge(*clipped(1))
                    nc.scalar.activation(lndp[:], clip[:], ACT.Ln).then_inc(logs.sem, 1)
                    nc.scalar.activation(mix_exp[:], mixes[:], ACT.Exp, bias=mix_nmax[:, 0:1]).then_inc(mixexp.sem, 1)
                    act.wait_ge(*biasmax(1))
                    nc.scalar.activation(pexp[:], pbT[:], ACT.Exp, bias=pb_nmax[:, 0:1]).then_inc(pbexp.sem, 1)
                    act.wait_ge(*logs(1))
                    for n in range(2):
                        nc.scalar.activation(power[:, n, :], dist[:], ACT.Exp, scale=lndp[:, n:n + 1]).then_inc(powers.sem, 1)
                    act.wait_ge(*esum_ready(1))
                    nc.scalar.activation(lse[:], esum[:], ACT.Ln).then_inc(lse_done.sem, 1)

                @block.tensor
                def _(pe):
                    pe.wait_ge(*loaded(16 * LOADS))
                    pe.wait_ge(*pbexp(1))
                    nc.tensor.transpose(bank[7][0:NOFF, 0:H], pexp[:], ident[0:H, 0:H]).then_inc(pexpT.sem, 1)
                    pe.wait_ge(*hot_ready(2))
                    for r in range(2):
                        for c, (a, b) in enumerate(cuts):
                            nc.tensor.matmul(bank[r * len(cuts) + c][0:96, 0:b - a], three[:], hot[:, r, a:b],
                                             start=True, stop=True).then_inc(sums.sem, 1)

        def spread_tables(sp):
            for dst, src, first, width in ((decay_t, decay_d, NEAR0, T), (decayb_t, decayb_d, 0, TABX),
                                           (biasr_t, biasr_d, 0, T), (bias_t, bias_d, 0, T)):
                sp.dma_start(dst, at(src, 127 + first, [[src.shape[1], H], [-1, P], [1, width]])).then_inc(tables_made.sem, 16)
            for g in range(G):
                sp.dma_start(biasp_t[g], at(biasp_d, (GH * g + GH - 1) * (PARTS * (T + 127)) + 127,
                                            [[T + 127, PARTS], [-1, P], [1, T]])).then_inc(tables_made.sem, 16)

        def norm_signals():
            return {n: sig("ln_" + n) for n in ("stats", "aggr", "std", "rstd", "norm", "transposed", "copied")}

        def close_norm(s):
            for n, total in (("stats", 1), ("aggr", 1), ("std", 1), ("rstd", 1),
                             ("norm", NCH + 1), ("transposed", NCH + 1), ("copied", NCH + 1)):
                s[n].close(total)

        def vector_statistics(v, s):
            for n in range(TILES):
                ins = nc.vector.bn_stats(stats[:, n, :], x_sb[:, n, :])
            ins.then_inc(s["stats"].sem, 1)
            v.wait_ge(*s["stats"](1))
            for n in range(TILES):
                ins = nc.vector.bn_aggr(meanvar[:, n, :], stats[:, n, :])
            ins.then_inc(s["aggr"].sem, 1)
            v.wait_ge(*s["std"](1))
            nc.vector.reciprocal(rstd[:, 0:TILES], rstd[:, 0:TILES]).then_inc(s["rstd"].sem, 1)
            v.wait_ge(*s["rstd"](1))

        def scalar_statistics(act, s):
            act.wait_ge(*s["aggr"](1))
            nc.scalar.activation(rstd[:, 0:TILES], meanvar[:, 0:TILES, 1], ACT.Sqrt,
                                 bias=eps[:, 0:1]).then_inc(s["std"].sem, 1)

        def vector_normalise(v, s, xn, c, slot):
            v.wait_ge(*s["transposed"](c - 1 if not isinstance(c, int) or c > 1 else 0))
            for k in range(TPC):
                tile = c * TPC + k
                ins = nc.vector.tensor_scalar(
                    xn[:, slot, k, :], x_sb[:, tile, :] if isinstance(c, int) else x_sb[:, bass.ds(tile, 1), :],
                    meanvar[:, tile, 0:1] if isinstance(c, int) else meanvar[:, bass.ds(tile, 1), 0],
                    rstd[:, tile:tile + 1] if isinstance(c, int) else rstd[:, bass.ds(tile, 1)],
                    ALU.subtract, ALU.mult)
            ins.then_inc(s["norm"].sem, 1)

        def tensor_transpose(pe, s, xn, c, slot):
            pe.wait_ge(*s["norm"](c + 1))
            pe.wait_ge(*s["copied"](c))
            for k in range(TPC):
                ins = nc.tensor.transpose(bank[0][:, k * P:(k + 1) * P], xn[:, slot, k, :], ident[:])
            ins.then_inc(s["transposed"].sem, 1)

        def project(cfg):
            rope, biased, gated = cfg["rope"], cfg["biased"], cfg["gated"]
            far = cfg["kind"] == "decay"
            NQ = 4 if rope else 2
            with ExitStack() as mem:
                w = sb("w", [P, cfg["nw"], P], where=mem)
                xn = sb("xn", [P, 2, TPC, D], where=mem)
                xTc = sb("xTc", [P, 2, CH], where=mem)
                b_qk = sb("b_qk", [P, 3], where=mem)
                b_q = sb("b_q", [P, 1], where=mem)
                b_v = sb("b_v", [P, P], where=mem)
                turn = sb("turn", [P, 4, T], where=mem) if rope else None
                full = sb("full", [P, 2, CH], where=mem)
                direct = sb("direct", [P, 2, CH], where=mem) if rope else None
                partner = sb("partner", [P, 2, CH], where=mem) if rope else None
                rest = sb("rest", [P, 2, 2, CH], where=mem)
                split = sb("split", [P, 2, 2, PARTS, CH], bf16, where=mem)
                factor = sb("factor", [P, 4, T], where=mem) if far else None
                far_full = sb("far_full", [P, 2, CH], where=mem) if far else None
                far_rest = sb("far_rest", [P, 2, CH], where=mem) if far else None
                far_split = sb("far_split", [P, 2, 2, PARTS, 2, CH], bf16, where=mem) if far else None
                far_made, far_hi, far_left, far_mid, far_lo = (sig("pj_far_product"), sig("pj_far_high"), sig("pj_far_rest"),
                                                               sig("pj_far_middle"), sig("pj_far_low"))
                ln = norm_signals()
                loaded, scaled = sig("pj_loaded"), sig("pj_bias_scaled")
                made = [sig(f"pj_product{i}") for i in range(NQ)]
                v_made, g_made = sig("pj_v_product"), sig("pj_gate_product")
                v_out, g_out = sig("pj_v_copied"), sig("pj_gate_done")
                turned = sig("pj_turned")
                f_ready, hi_ready = sig("pj_float_ready"), sig("pj_high_ready")
                r_ready, mid_ready, lo_ready = sig("pj_rest_ready"), sig("pj_middle_ready"), sig("pj_low_ready")
                stored = [sig("pj_stored0"), sig("pj_stored1")]
                def v_slot(b, half, k):
                    flat = V_sb[:, :, :, :, :].rearrange("p b g n c -> p b (g n c)")
                    tile = flat[:, bass.ds(b, 1), :].rearrange("p b (g n h d) -> p b g n h d", g=G, n=TPB, h=GH)
                    return tile[:, 0, :, half * TPC + k, :, 0:HD]

                block = mem.enter_context(nc.Block())
                nloads = 1 + 2 * biased + rope + G * far
                NSTORE = 2 * G * (1 + far)

                @block.sync
                def _(sp):
                    sp.dma_start(w[:], cfg["w"].rearrange("p (n f) -> p n f", f=P)).then_inc(loaded.sem, 16)
                    if biased:
                        sp.dma_start(b_qk[:], cfg["b_qk"]).then_inc(loaded.sem, 16)
                        sp.dma_start(b_v[:], cfg["b_v"].partition_broadcast(P)).then_inc(loaded.sem, 16)
                    if rope:
                        sp.dma_start(turn[:], t["turn"].rearrange("p (n f) -> p n f", f=T)).then_inc(loaded.sem, 16)
                    if far:
                        for g in range(G):
                            sp.dma_start(factor[LN_D * g:LN_D * (g + 1), :, :],
                                         at(far_d, g * (GH * 4 * T), [[0, HD], [4 * T, GH], [1, 4 * T]])).then_inc(loaded.sem, 16)
                    with sp.Fori(0, B) as b:
                        for half in range(2):
                            for n, dst in enumerate((q3_d, k3_d)):
                                sp.wait_ge(*lo_ready(4 * b + 2 * half + n + 1))
                                for g in range(G):
                                    sp.dma_start(
                                        at(dst, b * (PARTS * LN_D * T) + (g * B * PARTS * LN_D * T + half * CH),
                                           [[T, LN_D], [LN_D * T, PARTS], [1, CH]]),
                                        split[LN_D * g:LN_D * (g + 1), half, n, :, :]).then_inc(stored[half].sem, 16)
                            for n, dst in enumerate((q6_d, k6_d) if far else ()):
                                sp.wait_ge(*far_lo(8 * b + 4 * half + 2 * n + 2))
                                for g in range(G):
                                    sp.dma_start(
                                        at(dst, b * (PARTS * 2 * LN_D * T) + (g * B * PARTS * 2 * LN_D * T + half * CH),
                                           [[T, LN_D], [LN_D * T, PARTS * 2], [1, CH]]),
                                        far_split[LN_D * g:LN_D * (g + 1), half, n, :, :, :].rearrange("p a n t -> p (a n) t")).then_inc(stored[half].sem, 16)
                    for half in range(2):
                        sp.wait_ge(*stored[half](16 * NSTORE * B))

                @block.tensor
                def _(pe):
                    pe.wait_ge(*loaded(16 * nloads))
                    tensor_transpose(pe, ln, xn, 0, 0)
                    with pe.Fori(0, B) as b:
                        for half in range(2):
                            c = b * 2 + half
                            tensor_transpose(pe, ln, xn, c + 1, 1 - half)
                            pe.wait_ge(*ln["copied"](c + 1))
                            for i in range(NQ):
                                if rope:
                                    pe.wait_ge(*turned(2 * c))
                                else:
                                    pe.wait_ge(*f_ready(2 * c))
                                nc.tensor.matmul(bank[1 + i][:], w[:, i, :], xTc[:, half, :], start=True,
                                                 stop=True).then_inc(made[i].sem, 1)
                            pe.wait_ge(*v_out(c))
                            for k in range(TPC):
                                ins = nc.tensor.matmul(bank[5][:, k * P:(k + 1) * P], xTc[:, half, k * P:(k + 1) * P],
                                                       w[:, NQ, :], start=True, stop=True)
                            ins.then_inc(v_made.sem, 1)
                            if gated:
                                pe.wait_ge(*g_out(c))
                                nc.tensor.matmul(bank[6][:], w[:, NQ + 1, :], xTc[:, half, :], start=True,
                                                 stop=True).then_inc(g_made.sem, 1)

                @block.scalar
                def _(act):
                    scalar_statistics(act, ln)

                    def copy_transposed(c, slot):
                        act.wait_ge(*ln["transposed"](c + 1))
                        if not isinstance(c, int):
                            act.wait_ge(*(g_made if gated else v_made)(c - 1))
                        nc.scalar.activation(xTc[:, slot, :], bank[0][:], ACT.Copy).then_inc(ln["copied"].sem, 1)

                    act.wait_ge(*loaded(16 * nloads))
                    if biased:
                        act.wait_ge(*scaled(1))
                    copy_transposed(0, 0)
                    with act.Fori(0, B) as b:
                        for half in range(2):
                            c = b * 2 + half
                            copy_transposed(c + 1, 1 - half)
                            for n in range(2):
                                m = 2 * c + n
                                if not rope:
                                    act.wait_ge(*made[n](c + 1))
                                    act.wait_ge(*r_ready(2 * c))
                                    if far:
                                        act.wait_ge(*far_made(4 * c))
                                    if biased:
                                        ins = nc.scalar.activation(full[:, n, :], bank[1 + n][:], ACT.Identity,
                                                                   bias=(b_q[:, 0:1], b_qk[:, 1:2])[n],
                                                                   scale=(SCALE, 1.0)[n])
                                    else:
                                        ins = nc.scalar.activation(full[:, n, :], bank[1 + n][:], ACT.Copy,
                                                                   scale=(SCALE, 1.0)[n])
                                    ins.then_inc(f_ready.sem, 1)
                                act.wait_ge(*f_ready(m + 1))
                                act.wait_ge(*stored[half](b * (16 * NSTORE)))
                                nc.scalar.activation(split[:, half, n, 0, :], full[:, n, :], ACT.Copy).then_inc(hi_ready.sem, 1)
                            if not biased:
                                act.wait_ge(*v_made(c + 1))
                                for k in range(TPC):
                                    ins = nc.scalar.activation(v_slot(b, half, k),
                                                               bank[5][:, k * P:(k + 1) * P].rearrange("p (g h d) -> p g h d", g=G, h=GH), ACT.Copy)
                                ins.then_inc(v_out.sem, 1)
                            for k in range(4 if far else 0):
                                m = 4 * c + k
                                act.wait_ge(*far_made(m + 1))
                                nc.scalar.activation(far_split[:, half, k // 2, 0, k % 2, :], far_full[:, k % 2, :],
                                                     ACT.Copy).then_inc(far_hi.sem, 1)
                                act.wait_ge(*far_left(m + 1))
                                nc.scalar.activation(far_split[:, half, k // 2, 1, k % 2, :], far_rest[:, k % 2, :],
                                                     ACT.Copy).then_inc(far_mid.sem, 1)
                            if gated:
                                act.wait_ge(*g_made(c + 1))
                                nc.scalar.activation(gate_sb[0][:, bass.ds(c * CH, CH)], bank[6][:], ACT.Sigmoid,
                                                     bias=b_qk[:, 2:3]).then_inc(g_out.sem, 1)

                @block.vector
                def _(v):
                    vector_statistics(v, ln)
                    v.wait_ge(*loaded(16 * nloads))
                    if biased:
                        nc.vector.tensor_scalar(b_q[:], b_qk[:, 0:1], SCALE, None, ALU.mult).then_inc(scaled.sem, 1)
                    vector_normalise(v, ln, xn, 0, 0)
                    with v.Fori(0, B) as b:
                        for half in range(2):
                            c = b * 2 + half
                            vector_normalise(v, ln, xn, c + 1, 1 - half)
                            if rope:
                                for n in range(2):
                                    v.wait_ge(*f_ready(2 * c))
                                    for i, dst in ((n, direct), (n + 2, partner)):
                                        v.wait_ge(*made[i](c + 1))
                                        ins = nc.vector.tensor_tensor(dst[:, n, :], bank[1 + i][:],
                                                                      turn[:, i, half * CH:(half + 1) * CH], ALU.mult)
                                    ins.then_inc(turned.sem, 1)
                            if biased:
                                v.wait_ge(*v_made(c + 1))
                                for k in range(TPC):
                                    ins = nc.vector.tensor_tensor(v_slot(b, half, k),
                                                                  bank[5][:, k * P:(k + 1) * P].rearrange("p (g h d) -> p g h d", g=G, h=GH),
                                                                  b_v[:, :].rearrange("p (g h d) -> p g h d", g=G, h=GH), ALU.add)
                                ins.then_inc(v_out.sem, 1)
                            for n in range(2):
                                m = 2 * c + n
                                v.wait_ge(*hi_ready(m + 1))
                                nc.vector.tensor_tensor(rest[:, n, 0, :], full[:, n, :], split[:, half, n, 0, :],
                                                        ALU.subtract).then_inc(r_ready.sem, 1)
                                v.wait_ge(*r_ready(m + 1))
                                nc.vector.tensor_copy(split[:, half, n, 1, :], rest[:, n, 0, :]).then_inc(mid_ready.sem, 1)
                                v.wait_ge(*mid_ready(m + 1))
                                nc.vector.tensor_tensor(split[:, half, n, 2, :], rest[:, n, 0, :], split[:, half, n, 1, :],
                                                        ALU.subtract).then_inc(lo_ready.sem, 1)
                            for k in range(4 if far else 0):
                                m = 4 * c + k
                                v.wait_ge(*far_hi(m + 1))
                                v.wait_ge(*far_lo(4 * c + max(0, k - 1)))
                                nc.vector.tensor_tensor(far_rest[:, k % 2, :], far_full[:, k % 2, :], far_split[:, half, k // 2, 0, k % 2, :],
                                                        ALU.subtract).then_inc(far_left.sem, 1)
                                v.wait_ge(*far_mid(m + 1))
                                nc.vector.tensor_tensor(far_split[:, half, k // 2, 2, k % 2, :], far_rest[:, k % 2, :],
                                                        far_split[:, half, k // 2, 1, k % 2, :], ALU.subtract).then_inc(far_lo.sem, 1)

                if rope:
                    @block.gpsimd
                    def _(pool):
                        with pool.Fori(0, B) as b:
                            for half in range(2):
                                c = b * 2 + half
                                for n in range(2):
                                    pool.wait_ge(*turned(2 * c + n + 1))
                                    pool.wait_ge(*r_ready(2 * c))
                                    nc.gpsimd.tensor_tensor(full[:, n, :], direct[:, n, :], partner[:, n, :],
                                                            ALU.add).then_inc(f_ready.sem, 1)

                if far:
                    @block.gpsimd
                    def _(pool):
                        pool.wait_ge(*loaded(16 * nloads))
                        with pool.Fori(0, B) as b:
                            for half in range(2):
                                c = b * 2 + half
                                for k in range(4):
                                    if k % 2 == 0:
                                        pool.wait_ge(*f_ready(2 * c + k // 2 + 1))
                                    pool.wait_ge(*far_left(4 * c + max(0, k - 1)))
                                    nc.gpsimd.tensor_tensor(far_full[:, k % 2, :], full[:, k // 2, :],
                                                            factor[:, k, half * CH:(half + 1) * CH],
                                                            ALU.mult).then_inc(far_made.sem, 1)

            close_norm(ln)
            for s, n in ((far_made, 4 * NCH * far), (far_hi, 4 * NCH * far), (far_left, 4 * NCH * far),
                         (far_mid, 4 * NCH * far), (far_lo, 4 * NCH * far)):
                s.close(n)
            for s, n in ((loaded, 16 * nloads), (scaled, int(biased)), (v_made, NCH), (g_made, NCH * gated),
                         (v_out, NCH), (g_out, NCH * gated), (turned, 2 * NCH * rope), (f_ready, 2 * NCH),
                         (hi_ready, 2 * NCH), (r_ready, 2 * NCH), (mid_ready, 2 * NCH), (lo_ready, 2 * NCH),
                         (stored[0], 16 * NSTORE * B), (stored[1], 16 * NSTORE * B)):
                s.close(n)
            for s in made:
                s.close(NCH)

        def attend(cfg):
            kind = cfg["kind"]
            full = kind == "decay"
            adds = kind == "sparse"
            STEPS = G * B
            def key_tiles(I):
                if full:
                    return [(j % 2 ^ I) * TPC + j // 2 for j in range(TPB)]
                return [0] + [j for j in range(TPC * I, TPC * (I + 1)) if j] + list(range(1, TPC * I))

            units = [(I, j, 0 if full else max(0, P * j - CH * I)) for I in range(T // CH) for j in key_tiles(I)]
            U = len(units)
            far = [full and j // TPC != I for I, j, q0 in units]
            near = [(u, h) for u in range(U) for h in range(GH)
                    if kind != "causal" and not far[u] and not (adds and h == GH - 1)]
            NB = len(near)

            def changed(it, u, h):
                return it * NB + near.index((u, h)) + 1

            chunk_end = [u == U - 1 or units[u + 1][0] != units[u][0] for u in range(U)]
            diagonal = [] if kind != "causal" else [u for u, (I, j, q0) in enumerate(units) if j >= TPC * I]
            parts = [(h, i, m, min(CH, (T if full else P * (i + 1)) - CH * m))
                     for i in range(TPB) for h in range(GH) for m in range(T // CH) if full or P * (i + 1) > CH * m]
            NP = len(parts)
            UM = U - 2
            wide = [(CH - q0) * (3 if far[u] else 1) for u, (I, j, q0) in enumerate(units[:UM]) for h in range(GH)]
            slot_end, n = [], 0
            for k in range(len(wide)):
                due = sum(wide[:k + 1]) * sum(p[3] for p in parts) / sum(wide)
                while n < NP and sum(p[3] for p in parts[:n + 1]) <= due + 1e-6:
                    n += 1
                slot_end.append(n)
            assert n == NP

            def slot(u, h):
                k = u * GH + h
                return range(slot_end[k - 1] if k else 0, slot_end[k]) if u < UM else range(0)

            def ahead(k):
                if adds:
                    return slot_end[min(max(k, 0), len(slot_end) - 1)] if k >= 0 else 0
                done = slot_end[min(k, len(slot_end) - 1)] if k >= 0 else 0
                return min(slot_end[min(k + 1, len(slot_end) - 1)], done + 3)

            MW = TABX if full else T
            with ExitStack() as mem:
                QA = [sb(f"QA{i}", [ROWS + 1, GH, T], bf16, where=mem) for i in range(B)]
                KA = [sb(f"KA{i}", [ROWS + 1, GH, T], bf16, where=mem) for i in range(B)]
                QF = [sb(f"QF{i}", [FAR_ROWS + 1, GH, T], bf16, where=mem) for i in range(2 * full)]
                KF = [sb(f"KF{i}", [FAR_ROWS + 1, GH, T], bf16, where=mem) for i in range(2 * full)]
                Vt = [sb(f"Vt{i}", [P, TPB, GH * VW], where=mem) for i in range(B)]
                Ex = sb("Ex", [P, 2, GH, CH], where=mem)
                Ov = sb("Ov", [P, T // CH, CH], where=mem)
                mx = sb("mx", [P, GH * TPB, 2], where=mem)
                nmax = sb("nmax", [P, GH * TPB], where=mem)
                nrow = sb("nrow", [GH * TPB, P], bf16, where=mem)
                waste = sb("waste", [P, 2, CH], bf16, where=mem)
                ntab = GH if kind != "causal" else 1
                tab_m = sb("tab_m", [P, ntab, MW], bf16, where=mem)
                tab_e = sb("tab_e", [P, GH, T], where=mem) if kind != "causal" else None
                tab_p = sb("tab_p", [P, PARTS, T], bf16, where=mem) if adds else None
                ident_b = sb("ident_b", [P, P], bf16, where=mem) if adds else None
                pick = sb("pick", [ROWS + 1, P], bf16, where=mem) if full else None

                tabp, ident_made = sig("at_bias_parts"), sig("at_identity")
                far_ready = [sig(f"at_far_operands{i}") for i in range(2)]
                ready = [sig(f"at_operands{i}") for i in range(B)]
                once = sig("at_constants")
                filled = sig("at_filled")
                tabm, tabe = sig("at_max_table"), [sig(f"at_exp_table{h}") for h in range(GH)]
                m_scores, m_taken = sig("at_first_scores"), sig("at_maxima")
                m_seen, d_seen = sig("at_first_scores_seen"), sig("at_diagonal_seen")
                t_seen = sig("at_tables_unused_seen")
                n_ready, n_turned, n_copied, n_stored = (sig("at_negated"), sig("at_negated_turned"),
                                                         sig("at_negated_copied"), sig("at_negated_stored"))
                scores, biased, lowered, exped, masked = (sig("at_scores"), sig("at_scores_biased"),
                                                          sig("at_scores_lowered"), sig("at_exp"), sig("at_masked"))
                summed, o_out, o_stored = sig("at_values_summed"), sig("at_output_copied"), [sig("at_output_stored0"), sig("at_output_stored1")]
                block = mem.enter_context(nc.Block())
                NLOAD = 2 + PARTS
                NFAR = PARTS * 2
                NROW = 16 * (1 + full)
                NONCE = B + (kind == "causal") + 3 * full
                S_BANKS, M_BANKS, O_BANK = (0, 1, 2, 3), (4, 5, 6), 7

                def step_of(g, b):
                    return g * B + b

                def over_steps(eng, body):
                    with eng.Fori(0, G - 1) as g:
                        for b in range(B):
                            body(g, b, False)
                    for b in range(B):
                        body(G - 1, b, b == B - 1)

                @block.sync
                def _(sp):
                    def load(g, b):
                        it = step_of(g, b)
                        base = it * (PARTS * LN_D * T)
                        sp.dma_start(QA[b][0:ROWS, :, :], at(q3_d, base, [[0, PARTS], [GH * T, PARTS * HD], [1, GH * T]])).then_inc(ready[b].sem, 16)
                        for r in range(PARTS):
                            sp.dma_start(KA[b][r * PARTS * HD:(r + 1) * PARTS * HD, :, :],
                                         at(k3_d, base + r * (LN_D * T), [[0, PARTS], [GH * T, HD], [1, GH * T]])).then_inc(ready[b].sem, 16)
                        flat = V_sb[:, b, :, :, :].rearrange("p g n c -> p g (n c)")
                        sp.dma_start(Vt[b][:, :, :].rearrange("p n c -> p (n c)"),
                                     flat[:, g, :] if isinstance(g, int) else flat[:, bass.ds(g, 1), :]).then_inc(ready[b].sem, 16)

                    def load_far(g, b):
                        base = step_of(g, b) * (PARTS * 2 * LN_D * T)
                        row = 0
                        for r in range(PARTS):
                            rows = (PARTS - r) * 2 * HD
                            sp.dma_start(QF[b % 2][row:row + rows, :, :], at(q6_d, base, [[GH * T, rows], [1, GH * T]])).then_inc(far_ready[b % 2].sem, 16)
                            sp.dma_start(KF[b % 2][row:row + rows, :, :],
                                         at(k6_d, base + r * (2 * LN_D * T), [[0, PARTS - r], [GH * T, 2 * HD], [1, GH * T]])).then_inc(far_ready[b % 2].sem, 16)
                            row += rows

                    if kind == "causal":
                        sp.dma_start(tab_m[:, 0, :], t["causal"]).then_inc(once.sem, 16)
                    for i in range(B):
                        sp.dma_start(KA[i][ROWS:ROWS + 1, :, :], t["ones"]).then_inc(once.sem, 16)
                    if full:
                        sp.dma_start(pick[:], t["pick"]).then_inc(once.sem, 16)
                        for i in range(2):
                            sp.dma_start(KF[i][FAR_ROWS:FAR_ROWS + 1, :, :], t["ones"]).then_inc(once.sem, 16)

                    def load_tab_m(g):
                        for h in range(GH):
                            sp.dma_start(tab_m[:, h, :], at(decayb_t if full else biasr_t, (g * GH + h) * (P * MW),
                                                            [[MW, P], [1, MW]])).then_inc(tabm.sem, 16)

                    def load_tab_e(g):
                        if not isinstance(g, int) or g > 0:
                            sp.wait_ge(*biased(g * (B * NB)))
                            sp.sem_inc(t_seen.sem, 1)
                        for h in range(GH - adds):
                            sp.dma_start(tab_e[:, h, :], at(decay_t if full else bias_t, (g * GH + h) * (P * T),
                                                            [[T, P], [1, T]])).then_inc(tabe[h].sem, 16)
                        if adds:
                            if not isinstance(g, int) or g > 0:
                                sp.wait_ge(*scores(g * (B * U * GH)))
                                sp.sem_inc(t_seen.sem, 1)
                            sp.dma_start(tab_p[:], at(biasp_t, g * (PARTS * P * T), [[T, P], [P * T, PARTS], [1, T]])).then_inc(tabp.sem, 16)

                    def store_row(b, it):
                        sp.wait_ge(*n_copied(it + 1))
                        sp.dma_start(QA[b][ROWS:ROWS + 1, :, :], nrow[:]).then_inc(n_stored.sem, 16)
                        if full:
                            sp.dma_start(QF[b % 2][FAR_ROWS:FAR_ROWS + 1, :, :], nrow[:]).then_inc(n_stored.sem, 16)

                    load(0, 0)
                    if kind != "causal":
                        sp.wait_ge(*tables_made(16 * (4 + G)))
                        load_tab_m(0)
                        load_tab_e(0)
                    load(0, 1)
                    if full:
                        load_far(0, 0)
                        load_far(0, 1)
                    load(0, 2)
                    load(0, 3)
                    store_row(0, 0)

                    def body(g, b, last):
                        it = step_of(g, b)
                        more = not (isinstance(g, int) and g == G - 1)

                        def stores(I):
                            sp.wait_ge(*o_out(it * 2 + I + 1))
                            for h in range(GH):
                                sp.dma_start(at(ol_d, g * (GH * VW * T) + ((b * H + h) * VW * T + I * CH), [[T, VW], [1, CH]]),
                                             Ov[32 * h:32 * h + VW, I, :]).then_inc(o_stored[I].sem, 16)
                        stores(0)
                        if not last:
                            store_row((b + 1) % B, it + 1)
                        if more and b == B - 2 and kind != "causal":
                            load_tab_m(g + 1)
                        if more and b == B - 1 and kind != "causal":
                            load_tab_e(g + 1)
                        stores(1)
                        if more:
                            load(g + 1, b)
                        if full and (more or b < B - 2):
                            load_far(g + (b + 2) // B, (b + 2) % B)
                    over_steps(sp, body)
                    for I in range(2):
                        sp.wait_ge(*o_stored[I](16 * GH * STEPS))

                @block.tensor
                def _(pe):
                    def first_scores(g, b, some):
                        it = step_of(g, b)
                        for n in some:
                            h, i, m, width = parts[n]
                            pe.wait_ge(*m_taken(it * NP + max(0, n - 2)))
                            nc.tensor.matmul(bank[M_BANKS[n % 3]][:, 0:width], QA[b][0:ROWS, h, i * P:(i + 1) * P],
                                             KA[b][0:ROWS, h, m * CH:m * CH + width], start=True,
                                             stop=True).then_inc(m_scores.sem, 1)

                    def turn_maxima(it):
                        pe.wait_ge(*n_ready(it + 1))
                        nc.tensor.transpose(bank[M_BANKS[0]][0:GH * TPB, 0:P], nmax[:], ident[:]).then_inc(n_turned.sem, 1)

                    def values(g, b, u):
                        it = step_of(g, b)
                        I, j, q0 = units[u]
                        pe.wait_ge(*exped((it * U + u + 1) * GH))
                        if u in diagonal:
                            pe.wait_ge(*masked(it * len(diagonal) + diagonal.index(u) + 1))
                        first = u == 0 or chunk_end[u - 1]
                        if first:
                            pe.wait_ge(*o_out(it * 2 + I))
                        for h in range(GH):
                            ins = nc.tensor.matmul(bank[O_BANK][32 * h:32 * h + VW, q0:CH],
                                                   Vt[b][:, j, h * VW:(h + 1) * VW], Ex[:, u % 2, h, 0:CH - q0],
                                                   start=first, stop=chunk_end[u])
                        ins.then_inc(summed.sem, 1)

                    def second_scores(g, b, u, h):
                        it = step_of(g, b)
                        I, j, q0 = units[u]
                        n = (it * U + u) * GH + h
                        pe.wait_ge(*exped(n - GH + 1 if b > 0 or u > 0 else n - h))
                        K, Q, rows = (KF[b % 2], QF[b % 2], FAR_ROWS + 1) if far[u] else (KA[b], QA[b], ROWS + (not full))
                        by_pe = adds and h == GH - 1
                        ins = nc.tensor.matmul(bank[S_BANKS[h]][:, 0:CH - q0], K[0:rows, h, j * P:(j + 1) * P],
                                         Q[0:rows, h, I * CH + q0:(I + 1) * CH],
                                         start=True, stop=not by_pe)
                        if by_pe:
                            if b == 0 and u == 0:
                                pe.wait_ge(*tabp(g * 16 + 16))
                            c0 = CH * I + q0 - P * j
                            for r in range(PARTS):
                                ins = nc.tensor.matmul(bank[S_BANKS[h]][:, 0:CH - q0], ident_b[:], tab_p[:, r, c0:c0 + CH - q0],
                                                       start=False, stop=r == PARTS - 1)
                        ins.then_inc(scores.sem, 1)

                    def lower_scores(g, b, u, h):
                        it = step_of(g, b)
                        I, j, q0 = units[u]
                        pe.wait_ge(*biased(changed(it, u, h)))
                        nc.tensor.matmul(bank[S_BANKS[h]][:, :], pick[:], QA[b][0:ROWS + 1, h, I * CH:(I + 1) * CH],
                                         start=False, stop=True, skip_group_check=True).then_inc(lowered.sem, 1)

                    pe.wait_ge(*once(16 * NONCE))
                    pe.wait_ge(*ready[0](16 * NLOAD))
                    if adds:
                        pe.wait_ge(*ident_made(1))
                    first_scores(0, 0, range(NP))
                    turn_maxima(0)

                    def body(g, b, last):
                        it = step_of(g, b)
                        nb = (b + 1) % B
                        ng = g + 1 if nb == 0 else g
                        pe.wait_ge(*n_stored(NROW * (it + 1)))
                        if full:
                            pe.wait_ge(*far_ready[b % 2](g * (2 * 16 * NFAR) + (b // 2 + 1) * (16 * NFAR)))
                        pe.wait_ge(*filled(1))
                        if not last:
                            pe.wait_ge(*ready[nb]((ng + 1) * (16 * NLOAD)))
                        slots = [(u, h) for u in range(U) for h in range(GH)]
                        LAG = 2
                        if not last:
                            first_scores(ng, nb, range(ahead(-1)))
                        for k, (u, h) in enumerate(slots):
                            second_scores(g, b, u, h)
                            if not last:
                                first_scores(ng, nb, range(ahead(k - 1), ahead(k)))
                            if full and k >= LAG and not far[slots[k - LAG][0]]:
                                lower_scores(g, b, *slots[k - LAG])
                            if h == GH - 1:
                                if u > 0:
                                    values(g, b, u - 1)
                                if not last and u == UM:
                                    turn_maxima(it + 1)
                        if full:
                            for k in range(len(slots) - LAG, len(slots)):
                                if not far[slots[k][0]]:
                                    lower_scores(g, b, *slots[k])
                        values(g, b, U - 1)
                    over_steps(pe, body)

                @block.scalar
                def _(act):
                    def copy_row(it):
                        act.wait_ge(*n_turned(it + 1))
                        if not (isinstance(it, int) and it == 0):
                            act.wait_ge(*n_stored(NROW * it))
                        nc.scalar.activation(nrow[:], bank[M_BANKS[0]][0:GH * TPB, 0:P], ACT.Copy).then_inc(n_copied.sem, 1)

                    copy_row(0)

                    def copy_output(it, I):
                        act.wait_ge(*summed(it * U + max(n for n, x in enumerate(units) if x[0] == I) + 1))
                        if not (isinstance(it, int) and it == 0):
                            act.wait_ge(*o_stored[I](it * (16 * GH)))
                        nc.scalar.activation(Ov[:, I, :], bank[O_BANK][:], ACT.Copy).then_inc(o_out.sem, 1)

                    def body(g, b, last):
                        it = step_of(g, b)
                        for u in range(U):
                            I, j, q0 = units[u]
                            for h in range(GH):
                                n = (it * U + u) * GH + h
                                if (u, h) in near:
                                    act.wait_ge(*(lowered if full else biased)(changed(it, u, h)))
                                else:
                                    act.wait_ge(*scores(n + 1))
                                if h == 0 and b + u > 0:
                                    act.wait_ge(*summed(it * U + u - 1))
                                elif h == 0:
                                    act.wait_ge(*summed(it * U))
                                nc.scalar.activation(Ex[:, u % 2, h, 0:CH - q0], bank[S_BANKS[h]][:, 0:CH - q0],
                                                     ACT.Exp).then_inc(exped.sem, 1)
                            if u > 0 and chunk_end[u - 1]:
                                copy_output(it, 0)
                            if not last and u == UM:
                                copy_row(it + 1)
                        copy_output(it, 1)
                    over_steps(act, body)

                @block.vector
                def _(v):
                    nc.vector.memset(mx[:], NEG * 1e8)
                    nc.vector.memset(bank[O_BANK][:], 0.0).then_inc(filled.sem, 1)
                    v.wait_ge(*filled(1))
                    if adds:
                        nc.vector.tensor_copy(ident_b[:], ident[:]).then_inc(ident_made.sem, 1)
                    if kind == "causal":
                        v.wait_ge(*once(16 * NONCE))

                    def maxima(it, some):
                        for n in some:
                            h, i, m, width = parts[n]
                            if not (isinstance(it, int) and it == 0 and n < 2):
                                v.wait_ge(*m_taken(it * NP + n - 1))
                            v.wait_ge(*m_scores(it * NP + n + 1))
                            v.sem_inc(m_seen.sem, 1)
                            c0 = CH * m + (TPB - 1 - i) * P
                            tab = tab_m[:, h if kind != "causal" else 0, c0:c0 + width]
                            nc.vector.tensor_tensor_reduce(out=waste[:, n % 2, 0:width], in0=bank[M_BANKS[n % 3]][:, 0:width],
                                                           in1=tab, scale=1.0, scalar=NEG * 1e8,
                                                           op0=ALU.mult if full else ALU.add, op1=ALU.max,
                                                           accum_out=mx[:, h * TPB + i, m:m + 1]).then_inc(m_taken.sem, 1)

                    def negate(it):
                        v.wait_ge(*m_taken((it + 1) * NP))
                        if not (isinstance(it, int) and it == 0):
                            v.wait_ge(*n_turned(it))
                        nc.vector.tensor_reduce(nmax[:], mx[:], AX.X, ALU.max, negate=True).then_inc(n_ready.sem, 1)

                    if kind != "causal":
                        v.wait_ge(*tabm(16 * GH))
                    maxima(0, range(NP))
                    negate(0)

                    def body(g, b, last):
                        it = step_of(g, b)
                        nb = (b + 1) % B
                        if kind != "causal" and nb == 0 and not last:
                            v.wait_ge(*tabm((g + 2) * (16 * GH)))
                        for u in range(U):
                            I, j, q0 = units[u]
                            c0 = CH * I + q0 - P * j + (CH - P if full else 0)
                            for h in range(GH):
                                if b == 0 and (u, h) in near[0:GH - adds]:
                                    v.wait_ge(*tabe[h](g * 16 + 16))
                                if (u, h) in near:
                                    v.wait_ge(*scores((it * U + u) * GH + h + 1))
                                    s = bank[S_BANKS[h]][:, 0:CH - q0]
                                    nc.vector.tensor_tensor(s, s, tab_e[:, h, c0:c0 + CH - q0],
                                                            ALU.mult if full else ALU.add).then_inc(biased.sem, 1)
                                if not last:
                                    maxima(it + 1, slot(u, h))
                            if not last and u == UM - 1:
                                negate(it + 1)
                    over_steps(v, body)

                if diagonal:
                    @block.gpsimd
                    def _(pool):
                        def body(g, b, last):
                            it = step_of(g, b)
                            for k, u in enumerate(diagonal):
                                pool.wait_ge(*exped((it * U + u + 1) * GH))
                                pool.sem_inc(d_seen.sem, 1)
                                tile = Ex[:, u % 2, :, 0:P]
                                nc.gpsimd.affine_select(out=tile, in_=tile, compare_op=ALU.is_ge, fill=0.0, base=0,
                                                        pattern=[[0, GH], [1, P]], channel_multiplier=-1).then_inc(masked.sem, 1)
                        over_steps(pool, body)

            D8 = len(diagonal)
            other = kind != "causal"
            for s in ready:
                s.close(16 * NLOAD * G)
            for h, s in enumerate(tabe):
                s.close(16 * G * (other and not (adds and h == GH - 1)))
            tabp.close(16 * G * adds)
            ident_made.close(int(adds))
            for s in far_ready:
                s.close(16 * NFAR * (STEPS // 2) * full)
            for s, n in ((once, 16 * NONCE), (filled, 1), (tabm, 16 * GH * G * other), (m_scores, NP * STEPS), (m_taken, NP * STEPS),
                         (n_ready, STEPS), (n_turned, STEPS), (n_copied, STEPS), (n_stored, NROW * STEPS),
                         (scores, U * GH * STEPS), (biased, NB * STEPS), (lowered, NB * STEPS * full),
                         (exped, U * GH * STEPS), (masked, D8 * STEPS), (m_seen, NP * STEPS), (d_seen, D8 * STEPS), (t_seen, (G - 1) * (other + adds)), (summed, U * STEPS), (o_out, 2 * STEPS),
                         (o_stored[0], 16 * GH * STEPS), (o_stored[1], 16 * GH * STEPS)):
                s.close(n)

        def finish_attention(cfg):
            gated, biased = cfg["gated"], cfg["out_biased"]
            with ExitStack() as mem:
                den = sb("den", [P, CH], where=mem)
                inv = sb("inv", [P, CH], where=mem)
                w_o = sb("w_o", [P, P], where=mem)
                b_o = sb("b_o", [P, P], where=mem)
                O = sb("O", [P, B, T], where=mem)
                R = sb("R", [P, B, T], where=mem)
                loaded, den_in = sig("fa_loaded"), sig("fa_denominators")
                inverted, inv_stored = sig("fa_inverted"), sig("fa_inverses_stored")
                o_in = [sig(f"fa_output{b}") for b in range(B)]
                r_in = [sig(f"fa_inverses{b}") for b in range(B)]
                gated_s, normed = sig("fa_gated"), sig("fa_normalised")
                made, added, bias_added = sig("fa_product"), sig("fa_added"), sig("fa_bias_added")
                block = mem.enter_context(nc.Block())
                NL = 1 + biased

                @block.sync
                def _(sp):
                    sp.dma_start(den[:], at(ol_d, HD * T, [[VW * T, B * H], [CH, T // CH], [1, CH]])).then_inc(den_in.sem, 16)
                    sp.dma_start(w_o[:], cfg["w_o"]).then_inc(loaded.sem, 16)
                    if biased:
                        sp.dma_start(b_o[:], cfg["b_o"].partition_broadcast(P)).then_inc(loaded.sem, 16)
                    for b in range(B):
                        sp.dma_start(O[:, b, :], at(ol_d, b * (H * VW * T), [[VW * T, H], [T, HD], [1, T]])).then_inc(o_in[b].sem, 16)
                    sp.wait_ge(*inverted(1))
                    sp.dma_start(rl_d.rearrange("r (m n) -> (r m) n", n=CH), inv[:]).then_inc(inv_stored.sem, 16)
                    sp.wait_ge(*inv_stored(16))
                    for b in range(B):
                        sp.dma_start(R[:, b, :], at(rl_d, b * (H * T), [[T, H], [0, HD], [1, T]])).then_inc(r_in[b].sem, 16)

                @block.vector
                def _(v):
                    v.wait_ge(*den_in(16))
                    nc.vector.reciprocal(inv[:], den[:]).then_inc(inverted.sem, 1)

                    def add(b):
                        if biased:
                            v.wait_ge(*bias_added(B))
                        for c in range(T // CH):
                            n = b * 2 + c
                            v.wait_ge(*made(n + 1))
                            dst = x_sb[:, n * TPC:(n + 1) * TPC, :]
                            nc.vector.tensor_tensor(dst, dst, bank[n][:, :].rearrange("p (n f) -> p n f", f=D),
                                                    ALU.add).then_inc(added.sem, 1)

                    if gated:
                        for b in range(B):
                            v.wait_ge(*o_in[b](16))
                            nc.vector.tensor_tensor(O[:, b, :], O[:, b, :], gate_sb[0][:, b * T:(b + 1) * T],
                                                    ALU.mult).then_inc(gated_s.sem, 1)
                        v.wait_ge(*gated_s(B))
                    for b in range(B):
                        v.wait_ge(*o_in[b](16))
                        v.wait_ge(*r_in[b](16))
                        nc.vector.tensor_tensor(O[:, b, :], O[:, b, :], R[:, b, :], ALU.mult).then_inc(normed.sem, 1)
                        if b > 0:
                            add(b - 1)
                    add(B - 1)

                if biased:
                    @block.gpsimd
                    def _(pool):
                        pool.wait_ge(*loaded(16 * NL))
                        for b in range(B):
                            dst = x_sb[:, b * TPB:(b + 1) * TPB, :]
                            nc.gpsimd.tensor_tensor(dst, dst, b_o[:, :].unsqueeze(1).to_broadcast([P, TPB, D]),
                                                    ALU.add).then_inc(bias_added.sem, 1)

                @block.tensor
                def _(pe):
                    pe.wait_ge(*loaded(16 * NL))
                    for b in range(B):
                        pe.wait_ge(*normed(b + 1))
                        for c in range(T // CH):
                            for k in range(TPC):
                                q = c * CH + k * P
                                ins = nc.tensor.matmul(bank[b * 2 + c][:, k * P:(k + 1) * P], O[:, b, q:q + P], w_o[:],
                                                       start=True, stop=True)
                            ins.then_inc(made.sem, 1)

            for s in o_in + r_in:
                s.close(16)
            for s, n in ((loaded, 16 * NL), (den_in, 16), (inverted, 1), (inv_stored, 16),
                         (gated_s, B * gated), (normed, B), (made, 2 * B), (added, 2 * B),
                         (bias_added, B * biased)):
                s.close(n)

        def route(cfg, mem_xT, weight):
            shared = cfg["shared"]
            NR = E + shared
            with ExitStack() as mem:
                w_r = sb("w_r", [P, NR], where=mem)
                xn = sb("xn", [P, 2, TPC, D], where=mem)
                xTc = sb("xTc", [P, 2, CH], where=mem)
                logits = sb("logits", [P, TILES, NR], where=mem)
                top = sb("top", [P, 2, TILES], where=mem)
                place = sb("place", [P, 2, TILES], where=mem)
                second = sb("second", [P, TILES, E], where=mem)
                shifted = sb("shifted", [P, TILES, E], where=mem)
                hit = sb("hit", [P, 2, TILES, E], where=mem)
                number = sb("number", [P, E], where=mem)
                total = sb("total", [P, 2, TILES], where=mem)
                ln = norm_signals()
                loaded, made, kept = sig("ro_loaded"), sig("ro_logits"), sig("ro_logits_kept")
                xT_kept = sig("ro_transposed_kept")
                step, shift_ready, exp_ready = sig("ro_step"), sig("ro_shifted"), sig("ro_exp")
                block = mem.enter_context(nc.Block())

                @block.sync
                def _(sp):
                    sp.dma_start(w_r[:], cfg["w_r"]).then_inc(loaded.sem, 16)
                    sp.dma_start(number[:], t["number"].partition_broadcast(P)).then_inc(loaded.sem, 16)

                @block.tensor
                def _(pe):
                    pe.wait_ge(*loaded(32))
                    tensor_transpose(pe, ln, xn, 0, 0)
                    with pe.Fori(0, NCH // 2) as cc:
                        for half in range(2):
                            c = cc * 2 + half
                            tensor_transpose(pe, ln, xn, c + 1, 1 - half)
                            pe.wait_ge(*ln["copied"](c + 1))
                            pe.wait_ge(*kept(c))
                            for k in range(TPC):
                                ins = nc.tensor.matmul(bank[1][:, k * 16:k * 16 + NR], xTc[:, half, k * P:(k + 1) * P],
                                                       w_r[:], start=True, stop=True)
                            ins.then_inc(made.sem, 1)

                @block.scalar
                def _(act):
                    scalar_statistics(act, ln)

                    def copy_transposed(c, slot):
                        act.wait_ge(*ln["transposed"](c + 1))
                        if not isinstance(c, int):
                            act.wait_ge(*made(c - 1))
                            act.wait_ge(*xT_kept(c - 1))
                        nc.scalar.activation(xTc[:, slot, :], bank[0][:], ACT.Copy).then_inc(ln["copied"].sem, 1)
                    copy_transposed(0, 0)
                    with act.Fori(0, NCH // 2) as cc:
                        for half in range(2):
                            c = cc * 2 + half
                            copy_transposed(c + 1, 1 - half)
                            act.wait_ge(*ln["copied"](c + 1))
                            nc.scalar.activation(mem_xT[:, bass.ds(c * CH, CH)], xTc[:, half, :], ACT.Copy).then_inc(xT_kept.sem, 1)
                    act.wait_ge(*shift_ready(1))
                    nc.scalar.activation(shifted[:], shifted[:], ACT.Exp).then_inc(exp_ready.sem, 1)
                    if shared:
                        nc.scalar.activation(total[:, 1, :], logits[:, :, E], ACT.Exp, scale=-1.0).then_inc(exp_ready.sem, 1)

                @block.vector
                def _(v):
                    vector_statistics(v, ln)
                    vector_normalise(v, ln, xn, 0, 0)
                    with v.Fori(0, NCH // 2) as cc:
                        for half in range(2):
                            c = cc * 2 + half
                            vector_normalise(v, ln, xn, c + 1, 1 - half)
                            v.wait_ge(*made(c + 1))
                            nc.vector.tensor_copy(logits[:, bass.ds(c * TPC, TPC), :],
                                                  bank[1][:, 0:TPC * 16].rearrange("p (n f) -> p n f", f=16)[:, :, 0:NR]).then_inc(kept.sem, 1)
                    v.wait_ge(*kept(NCH))
                    v.wait_ge(*loaded(32))
                    done = [0]

                    def chained(ins):
                        done[0] += 1
                        ins.then_inc(step.sem, 1)
                        v.wait_ge(*step(done[0]))

                    wide = [P, TILES, E]
                    countdown = number[:, :].unsqueeze(1).to_broadcast(wide)
                    for n in range(2):
                        src = logits[:, :, 0:E] if n == 0 else second[:]
                        chained(nc.vector.tensor_reduce(top[:, n, :], src, AX.X, ALU.max))
                        if n == 0:
                            nc.vector.tensor_tensor(shifted[:], src, top[:, 0, :].unsqueeze(2).to_broadcast(wide),
                                                    ALU.subtract).then_inc(shift_ready.sem, 1)
                        chained(nc.vector.tensor_tensor(hit[:, n, :, :], src, top[:, n, :].unsqueeze(2).to_broadcast(wide),
                                                        ALU.is_equal))
                        chained(nc.vector.tensor_tensor(hit[:, n, :, :], hit[:, n, :, :], countdown, ALU.mult))
                        chained(nc.vector.tensor_reduce(place[:, n, :], hit[:, n, :, :], AX.X, ALU.max))
                        chained(nc.vector.tensor_tensor(hit[:, n, :, :], countdown,
                                                        place[:, n, :].unsqueeze(2).to_broadcast(wide), ALU.is_equal))
                        if n == 0:
                            chained(nc.vector.tensor_scalar(second[:], hit[:, 0, :, :], NEG, None, ALU.mult))
                            chained(nc.vector.tensor_tensor(second[:], second[:], logits[:, :, 0:E], ALU.add))
                    chained(nc.vector.tensor_tensor(hit[:, 0, :, :], hit[:, 0, :, :], hit[:, 1, :, :], ALU.add))
                    v.wait_ge(*exp_ready(1 + shared))
                    if shared:
                        chained(nc.vector.tensor_scalar(total[:, 1, :], total[:, 1, :], 1.0, None, ALU.add))
                        chained(nc.vector.reciprocal(weight[:, :, E], total[:, 1, :]))
                    chained(nc.vector.reduce_sum(total[:, 0, :], shifted[:], AX.X))
                    chained(nc.vector.reciprocal(total[:, 0, :], total[:, 0, :]))
                    chained(nc.vector.tensor_tensor(hit[:, 0, :, :], hit[:, 0, :, :], shifted[:], ALU.mult))
                    chained(nc.vector.tensor_tensor(weight[:, :, 0:E], hit[:, 0, :, :],
                                                    total[:, 0, :].unsqueeze(2).to_broadcast(wide), ALU.mult))
                    steps[0] = done[0]
            close_norm(ln)
            for s, n in ((loaded, 32), (made, NCH), (kept, NCH), (xT_kept, NCH), (step, steps[0]), (shift_ready, 1),
                         (exp_ready, 1 + shared)):
                s.close(n)

        steps = [0]

        def experts(cfg, xT, weight, spreads):
            shared = cfg["shared"]
            NR = E + shared
            NE = E + shared
            act_fn = ACT.Silu if shared else ACT.Gelu_apprx_tanh
            with ExitStack() as mem:
                w_up = sb("w_up", [P, E + 2 * shared, P], where=mem)
                w_down = sb("w_down", [P, NE, P], where=mem)
                b_up = sb("b_up", [P, E], where=mem)
                b_down = sb("b_down", [P, CH], where=mem)
                h = sb("h", [P, 2, CH], where=mem)
                gate = sb("gate", [P, CH], where=mem) if shared else None
                wst = sb("wst", [P, 2, P], where=mem)
                wT = sb("wT", [P, 2, P], where=mem)
                loaded, filled = sig("ex_loaded"), sig("ex_filled")
                up, active, down, added = sig("ex_up"), sig("ex_active"), sig("ex_down"), sig("ex_added")
                gated, up_shared, gate_done = sig("ex_gated"), sig("ex_up_shared"), sig("ex_gate")
                staged, turned, wT_ready, bias_made = sig("ex_weights_staged"), sig("ex_weights_turned"), sig("ex_weights_ready"), sig("ex_bias")
                block = mem.enter_context(nc.Block())
                NL = 2 if shared else 3 + TPC
                ADDS = NE * TPC + (not shared)
                H_BANKS, GATE_BANK, UP_BANK, Y_BANKS, B_BANK = (0, 1), 2, 3, (4, 5), 6

                @block.sync
                def _(sp):
                    sp.dma_start(w_up[:], cfg["w_up"].rearrange("p (e f) -> p e f", f=P)).then_inc(loaded.sem, 16)
                    sp.dma_start(w_down[:], cfg["w_down"].rearrange("p (e f) -> p e f", f=P)).then_inc(loaded.sem, 16)
                    if not shared:
                        sp.dma_start(b_up[:], cfg["b_up"]).then_inc(loaded.sem, 16)
                        sp.wait_ge(*filled(1))
                        for k in range(TPC):
                            sp.dma_start(b_down[k * E:(k + 1) * E, k * P:(k + 1) * P], cfg["b_down"]).then_inc(loaded.sem, 16)
                    if spreads:
                        spread_tables(sp)

                if not shared:
                    @block.gpsimd
                    def _(pool):
                        nc.gpsimd.memset(b_down[:], 0.0).then_inc(filled.sem, 1)
                        nc.gpsimd.memset(wst[:], 0.0).then_inc(filled.sem, 1)
                        pool.wait_ge(*filled(2))
                        with pool.Fori(0, NCH // 2) as cc:
                            for half in range(2):
                                c = cc * 2 + half
                                pool.wait_ge(*turned(cc * 2))
                                nc.gpsimd.tensor_copy(wst[:, half, 0:TPC * E].rearrange("p (n e) -> p n e", e=E),
                                                      weight[:, bass.ds(c * TPC, TPC), 0:E]).then_inc(staged.sem, 1)

                @block.tensor
                def _(pe):
                    pe.wait_ge(*loaded(16 * NL))

                    def down_products(c, half, e):
                        d = half * NE + e
                        pe.wait_ge(*(active(c * E + e + 1) if e < E else gated(c + 1)))
                        pe.wait_ge(*added_before(c, half, e))
                        for k in range(TPC):
                            ins = nc.tensor.matmul(bank[Y_BANKS[d % 2]][:, k * P:(k + 1) * P],
                                                   h[:, d % 2, k * P:(k + 1) * P], w_down[:, e, :], start=True, stop=True)
                        ins.then_inc(down.sem, 1)

                    def added_before(c, half, e):
                        if e >= 2:
                            return added(c * ADDS + (e - 1) * TPC)
                        return added(c * ADDS if half == 0 else c * ADDS - (not shared) - (1 - e) * TPC)

                    with pe.Fori(0, NCH // 2) as cc:
                        for half in range(2):
                            c = cc * 2 + half
                            moving = xT[:, bass.ds(c * CH, CH)]
                            for e in range(NE):
                                if e < E:
                                    pe.wait_ge(*active(c * E + (e - 1 if e >= 2 else 0)))
                                    nc.tensor.matmul(bank[H_BANKS[e % 2]][:], w_up[:, e, :], moving, start=True,
                                                     stop=True).then_inc(up.sem, 1)
                                else:
                                    pe.wait_ge(*gated(c))
                                    for i, bk in ((E, GATE_BANK), (E + 1, UP_BANK)):
                                        ins = nc.tensor.matmul(bank[bk][:], w_up[:, i, :], moving, start=True, stop=True)
                                    ins.then_inc(up_shared.sem, 1)
                                if e > 0:
                                    down_products(c, half, e - 1)
                                if e == 3 and not shared:
                                    pe.wait_ge(*staged(c + 1))
                                    pe.wait_ge(*added(c * ADDS))
                                    nc.tensor.transpose(bank[B_BANK][:, 0:P], wst[:, half, :], ident[:]).then_inc(turned.sem, 1)
                                if e == 6 and not shared:
                                    pe.wait_ge(*wT_ready(c + 1))
                                    nc.tensor.matmul(bank[B_BANK][:], wT[:, half, :], b_down[:], start=True,
                                                     stop=True).then_inc(bias_made.sem, 1)
                            down_products(c, half, NE - 1)

                @block.scalar
                def _(act):
                    act.wait_ge(*loaded(16 * NL))
                    with act.Fori(0, NCH // 2) as cc:
                        for half in range(2):
                            c = cc * 2 + half
                            for e in range(E):
                                n, d = c * NE + e, half * NE + e
                                act.wait_ge(*up(c * E + e + 1))
                                act.wait_ge(*down(n - 1 if e >= 2 or half else c * NE))
                                if shared:
                                    ins = nc.scalar.activation(h[:, d % 2, :], bank[H_BANKS[e % 2]][:], act_fn)
                                else:
                                    ins = nc.scalar.activation(h[:, d % 2, :], bank[H_BANKS[e % 2]][:], act_fn,
                                                               bias=b_up[:, e:e + 1])
                                ins.then_inc(active.sem, 1)
                                if e == 4 and not shared:
                                    act.wait_ge(*turned(c + 1))
                                    act.wait_ge(*bias_made(c))
                                    nc.scalar.activation(wT[:, half, :], bank[B_BANK][:, 0:P], ACT.Copy).then_inc(wT_ready.sem, 1)
                            if shared:
                                act.wait_ge(*up_shared(c + 1))
                                act.wait_ge(*gated(c))
                                nc.scalar.activation(gate[:], bank[GATE_BANK][:], act_fn).then_inc(gate_done.sem, 1)

                @block.vector
                def _(v):
                    with v.Fori(0, NCH // 2) as cc:
                        for half in range(2):
                            c = cc * 2 + half
                            x_c = [x_sb[:, bass.ds(c * TPC + k, 1), :] for k in range(TPC)]
                            for e in range(NE):
                                d = half * NE + e
                                if e == E:
                                    v.wait_ge(*gate_done(c + 1))
                                    v.wait_ge(*down(c * NE + E - 1))
                                    nc.vector.tensor_tensor(h[:, d % 2, :], gate[:], bank[UP_BANK][:],
                                                            ALU.mult).then_inc(gated.sem, 1)
                                v.wait_ge(*down(c * NE + e + 1))
                                for k in range(TPC):
                                    if e > 0:
                                        v.wait_ge(*added(c * ADDS + (e - 1) * TPC + k + 1))
                                    nc.vector.scalar_tensor_tensor(out=x_c[k], in0=bank[Y_BANKS[d % 2]][:, k * P:(k + 1) * P].unsqueeze(1),
                                                                   scalar=weight[:, bass.ds(c * TPC + k, 1), e], in1=x_c[k],
                                                                   op0=ALU.mult, op1=ALU.add).then_inc(added.sem, 1)
                            if not shared:
                                v.wait_ge(*added(c * ADDS + NE * TPC))
                                v.wait_ge(*bias_made(c + 1))
                                dst = x_sb[:, bass.ds(c * TPC, TPC), :]
                                nc.vector.tensor_tensor(dst, dst, bank[B_BANK][:, :].rearrange("p (n f) -> p n f", f=D),
                                                        ALU.add).then_inc(added.sem, 1)
            for s, n in ((loaded, 16 * NL), (filled, 2 * (not shared)), (up, NCH * E), (active, NCH * E), (gated, NCH * shared), (down, NCH * NE),
                         (added, NCH * ADDS), (up_shared, NCH * shared), (gate_done, NCH * shared),
                         (staged, NCH * (not shared)), (turned, NCH * (not shared)), (wT_ready, NCH * (not shared)),
                         (bias_made, NCH * (not shared))):
                s.close(n)

        def epilogue():
            with ExitStack() as mem:
                stored = sig("x_stored")
                block = mem.enter_context(nc.Block())

                @block.sync
                def _(sp):
                    sp.dma_start(out.rearrange("(n p) f -> p n f", p=P), x_sb[:, 0:TILES, :]).then_inc(stored.sem, 16)
                    sp.wait_ge(*stored(16))

        gate_sb = [None]

        def attention(cfg):
            with ExitStack() as mem:
                if cfg["gated"]:
                    gate_sb[0] = sb("gate_sb", [P, B * T], where=mem)
                project(cfg)
                attend(cfg)
                finish_attention(cfg)

        def moe(cfg, spreads):
            with ExitStack() as mem:
                xT = sb("xT", [P, B * T], where=mem)
                weight = sb("weight", [P, TILES, E + 1], where=mem)
                route(cfg, xT, weight)
                experts(cfg, xT, weight, spreads)

        attentions = [
            dict(kind="causal", rope=False, biased=False, gated=False, out_biased=True, w=t["w0"], nw=3,
                 w_o=t["wo0"], b_o=t["bo0"]),
            dict(kind="decay", rope=False, biased=True, gated=False, out_biased=True, w=t["w1"], nw=3,
                 b_qk=t["bqk1"], b_v=t["bv1"], w_o=t["wo1"], b_o=t["bo1"]),
            dict(kind="sparse", rope=False, biased=True, gated=True, out_biased=True, w=t["w2"], nw=4,
                 b_qk=t["bqk2"], b_v=t["bv2"], w_o=t["wo2"], b_o=t["bo2"]),
            dict(kind="causal", rope=True, biased=False, gated=False, out_biased=False, w=t["w3"], nw=5,
                 w_o=t["wo3"]),
        ]
        ffn0 = dict(shared=0, w_r=t["wr0"], w_up=t["wup0"], w_down=t["wdn0"], b_up=t["bup0"], b_down=t["bdn0"])
        ffn1 = dict(shared=1, w_r=t["wr1"], w_up=t["wup1"], w_down=t["wdn1"])

        prologue()
        for n, ffn in enumerate((ffn0, ffn0, ffn1, ffn1)):
            attention(attentions[n])
            moe(ffn, spreads=n == 0)
        epilogue()


def kernel(**inputs):
    import numpy as np
    import concourse.bacc as bacc
    from concourse.bass_utils import run_bass_kernel_spmd

    def get(name):
        return np.asarray(inputs[name])

    perm = np.array([(GH * g + h) * HD + d for g in range(G) for d in range(HD) for h in range(GH)])
    swap = np.array([(GH * g + h) * HD + (d ^ 1) for g in range(G) for d in range(HD) for h in range(GH)])

    def side_by_side(*parts):
        return np.ascontiguousarray(np.concatenate(parts, axis=1))

    def column(*rows):
        return np.ascontiguousarray(np.stack(rows, axis=1))

    def experts(w):
        return np.ascontiguousarray(w.transpose(1, 0, 2).reshape(P, -1))

    f32, half_type = np.float32, mybir.dt.np(bf16)
    a = {}
    a["x"] = np.ascontiguousarray(get("L0_attn_a_x").reshape(B * T, D))
    a["ident"] = np.eye(P, dtype=f32)
    cols = np.arange(T) - (T - P)
    a["causal"] = np.where(cols[None, :] > np.arange(P)[:, None], f32(NEG), f32(0)).astype(half_type)
    a["ones"] = np.ones((1, GH * T), dtype=half_type)
    pick = np.zeros((ROWS + 1, P), dtype=f32)
    pick[ROWS] = 1
    a["pick"] = pick.astype(half_type)
    a["dist"] = np.abs(np.arange(ROWX) - (T - 1)).astype(f32)[None, :]
    a["delta"] = (np.arange(T + 127) - 127).astype(f32)[None, :]
    a["deltar"] = (T - 1 - np.arange(T + 127)).astype(f32)[None, :]
    a["number"] = (E - np.arange(E)).astype(f32)[None, :]
    inv_freq = (f32(1) / (f32(10000) ** (np.arange(0, HD, 2).astype(f32) / f32(HD)))).astype(f32)
    angle = (np.arange(T).astype(f32)[:, None] * inv_freq[None, :]).astype(f32).astype(np.float64)
    dims = np.array([d for g in range(G) for d in range(HD) for h in range(GH)])
    cos = np.cos(angle)[:, dims // 2].T
    sin = (np.sin(angle)[:, dims // 2] * np.where(dims % 2, 1.0, -1.0)[None, :]).T
    a["turn"] = np.ascontiguousarray(np.concatenate([cos * SCALE, cos, sin * SCALE, sin], axis=1).astype(f32))
    wq, wk, wv = np.split(get("L0_attn_a_w_qkv"), 3, axis=1)
    a["w0"] = side_by_side(wq[:, perm], wk[:, perm], wv)
    a["wo0"], a["bo0"] = get("L0_attn_a_w_out"), get("L0_attn_a_b_out")[None, :]
    a["w1"] = side_by_side(get("L0_attn_b_Wq").T[:, perm], get("L0_attn_b_Wk").T[:, perm], get("L0_attn_b_Wv").T)
    bq, bk = get("L0_attn_b_bq"), get("L0_attn_b_bk")
    a["bqk1"] = column(bq[perm], bk[perm], bk)
    a["bv1"] = get("L0_attn_b_bv")[None, :]
    a["wo1"], a["bo1"] = np.ascontiguousarray(get("L0_attn_b_Wo").T), get("L0_attn_b_bo")[None, :]
    a["decay"], a["mix"] = get("L0_attn_b_decay_params"), get("L0_attn_b_mix_weights")
    wq, wk, wv = np.split(get("L1_attn_a_Wqkv").T, 3, axis=1)
    bq, bk, bv = np.split(get("L1_attn_a_bqkv"), 3)
    a["w2"] = side_by_side(wq[:, perm], wk[:, perm], wv, get("L1_attn_a_Wgate").T)
    a["bqk2"] = column(bq[perm], bk[perm], get("L1_attn_a_bgate"))
    a["bv2"] = bv[None, :]
    a["wo2"], a["bo2"] = np.ascontiguousarray(get("L1_attn_a_Wout").T), get("L1_attn_a_bout")[None, :]
    a["pos_bias"] = get("L1_attn_a_pos_bias")
    a["pos_biasT"] = np.ascontiguousarray(a["pos_bias"].T)
    a["offsets"] = get("L1_attn_a_offsets")[:, None]
    q, k = get("L1_attn_b_qw"), get("L1_attn_b_kw")
    a["w3"] = side_by_side(q[:, perm], k[:, perm], q[:, swap], k[:, swap], get("L1_attn_b_vw"))
    a["wo3"] = get("L1_attn_b_ow")
    a["wr0"] = get("L0_ffn_router_w")
    a["wup0"], a["wdn0"] = experts(get("L0_ffn_w_in")), experts(get("L0_ffn_w_out"))
    a["bup0"], a["bdn0"] = np.ascontiguousarray(get("L0_ffn_b_in").T), get("L0_ffn_b_out")
    a["wr1"] = side_by_side(get("L1_ffn_router_w"), get("L1_ffn_shared_gate_w"))
    a["wup1"] = side_by_side(experts(get("L1_ffn_w1")), get("L1_ffn_shared_gate_up"))
    a["wdn1"] = side_by_side(experts(get("L1_ffn_w2")), get("L1_ffn_shared_down"))

    nc = bacc.Bacc("TRN2", target_bir_lowering=False, num_devices=1)
    arrays, tensors = {}, {}
    for name, value in a.items():
        value = np.ascontiguousarray(value)
        arrays[f"in_{name}"] = value
        tensors[name] = nc.dram_tensor(f"in_{name}", value.shape, mybir.dt.from_np(value.dtype), kind="ExternalInput").ap()
    out = nc.dram_tensor("out_x", (B * T, D), fp32, kind="ExternalOutput").ap()
    hybrid_program(nc, tensors, out)
    r = run_bass_kernel_spmd(nc, [arrays], core_ids=[0])
    return r.results[0]["out_x"].reshape(B, T, D)
```
